# Optimizing a Trainium2 kernel written in Bass

```python
import numpy as np
import jax
import jax.numpy as jnp

def _softmax(x, axis=-1):
    return jax.nn.softmax(x, axis=axis)

def _gelu(x):
    return jax.nn.gelu(x, approximate=True)

def _silu(x):
    return jax.nn.silu(x)

def _sigmoid(x):
    return jax.nn.sigmoid(x)

def _layernorm(x, axis=-1, eps=1e-05):
    m = jnp.mean(x, axis=axis, keepdims=True)
    v = jnp.var(x, axis=axis, keepdims=True)
    return (x - m) / jnp.sqrt(v + eps)

def _scatter_add(tgt, idx, src, axis=0):
    return tgt.at[idx].add(src)

def _segment_sum(src, seg, n):
    return jax.ops.segment_sum(src, seg, n)
kernel_name = 'mk_adaln_ffn_d2_seqx_r8_82e8f0'

def setup_inputs(seed: int=0):
    np.random.seed(seed)
    _w = jnp.asarray

    def _rec_inputs():
        import jax
        import jax.numpy as jnp
        _rk = jax.random.key(seed)
        x = -0.000125 + 0.9999 * jax.random.normal(jax.random.fold_in(_rk, 1), (8, 128, 512), jnp.float32)
        _lenS = 128 - jax.random.randint(jax.random.fold_in(_rk, 7), (8,), 0, max(1, 128 // 4) + 1, jnp.int32)
        _lenS2 = 128 - jax.random.randint(jax.random.fold_in(_rk, 8), (8,), 0, max(1, 128 // 4) + 1, jnp.int32)
        itok_B_0_7 = jax.random.randint(jax.random.fold_in(_rk, 11), (8,), 0, 8, jnp.int32)
        itok_B_3_7 = jax.random.randint(jax.random.fold_in(_rk, 12), (8,), 3, 8, jnp.int32)
        return (x, itok_B_0_7, itok_B_3_7)
    x, itok_B_0_7, itok_B_3_7 = _rec_inputs()

    def _L0_cond_setup():
        import jax, jax.numpy as jnp
        import numpy as np
        TOP_K = 2
        LANG_BIAS = 5.0
        SCALING = 32.0 / 16.0
        LANGUAGE_PAD_ID = -1
        key = jax.random.key(seed)
        ks = jax.random.split(key, 6)
        B, T, D, O, E, R = (4, 256, 512, 512, 8, 16)
        x = jax.random.normal(ks[0], (B, T, D), dtype=jnp.float32)
        language_ids = jax.random.randint(ks[1], (B,), 0, E).astype(jnp.int64)
        W = jax.random.normal(ks[2], (O, D), dtype=jnp.float32) * (1.0 / np.sqrt(D))
        Wr = jax.random.normal(ks[3], (E, D), dtype=jnp.float32) * (1.0 / np.sqrt(D))
        A = jax.random.normal(ks[4], (E, R, D), dtype=jnp.float32) * (1.0 / np.sqrt(D))
        Bm = jax.random.normal(ks[5], (O, R), dtype=jnp.float32) * 0.0
        Bm = jnp.broadcast_to(Bm, (E, O, R)) + jax.random.normal(ks[5], (E, O, R), dtype=jnp.float32) * 0.02
        return {'x': x, 'language_ids': language_ids, 'W': W, 'Wr': Wr, 'A': A, 'B': Bm}
    _L0_cond_all = _L0_cond_setup()
    _L0_cond_in = {k: v for k, v in _L0_cond_all.items() if k in ('W', 'Wr', 'A', 'B')}
    del _L0_cond_all

    def _L0_ffn_setup():
        import jax, jax.numpy as jnp
        import numpy as np
        HIDDEN = 512
        INTER = 1376
        GROUP = 128
        B, S = (4, 256)
        NIB = jnp.uint32(15)

        def _pack_rows(nib):
            r = nib.reshape(-1, 8, nib.shape[-1])
            shifts = (jnp.arange(8, dtype=jnp.uint32) * 4)[None, :, None]
            return jnp.sum(r << shifts, axis=1, dtype=jnp.uint32)

        def _pack_cols(nib):
            r = nib.reshape(nib.shape[0], -1, 8)
            shifts = (jnp.arange(8, dtype=jnp.uint32) * 4)[None, None, :]
            return jnp.sum(r << shifts, axis=2, dtype=jnp.uint32)

        def _dequant(qw, qz, sc, g_idx):
            shifts = jnp.arange(8, dtype=jnp.uint32) * 4
            wq = qw[:, None, :] >> shifts[None, :, None] & NIB
            wq = wq.reshape(-1, qw.shape[1]).astype(jnp.float32)
            zq = qz[:, :, None] >> shifts[None, None, :] & NIB
            zq = zq.reshape(qz.shape[0], -1).astype(jnp.float32) + 1.0
            return sc[g_idx] * (wq - zq[g_idx])
        key = jax.random.key(seed)
        ks = jax.random.split(key, 7)
        n_groups = HIDDEN // GROUP
        n_groups_d = INTER // GROUP
        x = jax.random.normal(ks[0], (B, S, HIDDEN), jnp.float32)
        nib_w_gu = jax.random.randint(ks[1], (HIDDEN, 2 * INTER), 0, 16).astype(jnp.uint32)
        nib_z_gu = jax.random.randint(ks[2], (n_groups, 2 * INTER), 0, 15).astype(jnp.uint32)
        qweight_gu = _pack_rows(nib_w_gu)
        qzeros_gu = _pack_cols(nib_z_gu)
        scales_gu = jax.random.uniform(ks[3], (n_groups, 2 * INTER), jnp.float32, 0.005, 0.02)
        g_idx_gu = jnp.arange(HIDDEN, dtype=jnp.int32) // GROUP
        nib_w_d = jax.random.randint(ks[4], (INTER, HIDDEN), 0, 16).astype(jnp.uint32)
        nib_z_d = jax.random.randint(ks[5], (n_groups_d, HIDDEN), 0, 15).astype(jnp.uint32)
        qweight_down = _pack_rows(nib_w_d)
        qzeros_down = _pack_cols(nib_z_d)
        scales_down = jax.random.uniform(ks[6], (n_groups_d, HIDDEN), jnp.float32, 0.005, 0.02)
        g_idx_down = jnp.arange(INTER, dtype=jnp.int32) // GROUP
        return {'x': x, 'qweight_gu': qweight_gu, 'qzeros_gu': qzeros_gu, 'scales_gu': scales_gu, 'g_idx_gu': g_idx_gu, 'qweight_down': qweight_down, 'qzeros_down': qzeros_down, 'scales_down': scales_down, 'g_idx_down': g_idx_down}
    _L0_ffn_all = _L0_ffn_setup()
    _L0_ffn_in = {k: v for k, v in _L0_ffn_all.items() if k in ('qweight_gu', 'qzeros_gu', 'scales_gu', 'g_idx_gu', 'qweight_down', 'qzeros_down', 'scales_down', 'g_idx_down')}
    del _L0_ffn_all

    def _L1_cond_setup():
        import jax, jax.numpy as jnp
        import numpy as np
        MAX_LORAS, OUT, IN = (8, 512, 512)
        B, S = (4, 256)
        key = jax.random.key(seed)
        k1, k2, k3 = jax.random.split(key, 3)
        x = jax.random.normal(k1, (B, S, IN), dtype=jnp.float32)
        weight = jax.random.normal(k2, (MAX_LORAS, OUT, IN), dtype=jnp.float32) * 0.02
        adapter_ids = jax.random.randint(k3, (B,), 0, MAX_LORAS, dtype=jnp.int32)
        return {'x': x, 'weight': weight, 'adapter_ids': adapter_ids}
    _L1_cond_all = _L1_cond_setup()
    _L1_cond_in = {k: v for k, v in _L1_cond_all.items() if k in ('weight',)}
    del _L1_cond_all

    def _L1_ffn_setup():
        import jax, jax.numpy as jnp
        import numpy as np
        RMS_EPS = 1e-05
        key = jax.random.key(seed)
        k1, k2, k3, k4 = jax.random.split(key, 4)
        B, S, H, I = (1, 256, 512, 1792)
        x = jax.random.normal(k1, (B, S, H), dtype=jnp.float32)
        ln_w = jnp.ones((H,), dtype=jnp.float32)
        gate_w = jax.random.normal(k2, (I, H), dtype=jnp.float32) * 0.02
        up_w = jax.random.normal(k3, (I, H), dtype=jnp.float32) * 0.02
        down_w = jax.random.normal(k4, (H, I), dtype=jnp.float32) * 0.02
        return {'x': x, 'ln_w': ln_w, 'gate_w': gate_w, 'up_w': up_w, 'down_w': down_w}
    _L1_ffn_all = _L1_ffn_setup()
    _L1_ffn_in = {k: v for k, v in _L1_ffn_all.items() if k in ('ln_w', 'gate_w', 'up_w', 'down_w')}
    del _L1_ffn_all
    return {'x': x, 'itok_B_0_7': itok_B_0_7, 'itok_B_3_7': itok_B_3_7, 'L0_cond_W': _L0_cond_in['W'], 'L0_cond_Wr': _L0_cond_in['Wr'], 'L0_cond_A': _L0_cond_in['A'], 'L0_cond_B': _L0_cond_in['B'], 'L0_ffn_qweight_gu': _L0_ffn_in['qweight_gu'], 'L0_ffn_qzeros_gu': _L0_ffn_in['qzeros_gu'], 'L0_ffn_scales_gu': _L0_ffn_in['scales_gu'], 'L0_ffn_g_idx_gu': _L0_ffn_in['g_idx_gu'], 'L0_ffn_qweight_down': _L0_ffn_in['qweight_down'], 'L0_ffn_qzeros_down': _L0_ffn_in['qzeros_down'], 'L0_ffn_scales_down': _L0_ffn_in['scales_down'], 'L0_ffn_g_idx_down': _L0_ffn_in['g_idx_down'], 'L1_cond_weight': _L1_cond_in['weight'], 'L1_ffn_ln_w': _L1_ffn_in['ln_w'], 'L1_ffn_gate_w': _L1_ffn_in['gate_w'], 'L1_ffn_up_w': _L1_ffn_in['up_w'], 'L1_ffn_down_w': _L1_ffn_in['down_w']}

def reference(x, itok_B_0_7, itok_B_3_7, L0_cond_W, L0_cond_Wr, L0_cond_A, L0_cond_B, L0_ffn_qweight_gu, L0_ffn_qzeros_gu, L0_ffn_scales_gu, L0_ffn_g_idx_gu, L0_ffn_qweight_down, L0_ffn_qzeros_down, L0_ffn_scales_down, L0_ffn_g_idx_down, L1_cond_weight, L1_ffn_ln_w, L1_ffn_gate_w, L1_ffn_up_w, L1_ffn_down_w):
    import jax
    import jax.numpy as jnp

    def _L0_cond_ref(x, language_ids, W, Wr, A, B):
        import jax, jax.numpy as jnp
        import numpy as np
        TOP_K = 2
        LANG_BIAS = 5.0
        SCALING = 32.0 / 16.0
        LANGUAGE_PAD_ID = -1
        base = jnp.einsum('btd,od->bto', x, W)
        E = Wr.shape[0]
        logits = jnp.einsum('btd,ed->bte', x.astype(jnp.float32), Wr.astype(jnp.float32))
        expert_targets = language_ids
        valid = expert_targets >= 0
        tgt = jnp.where(valid, expert_targets, 0)
        bias = jax.nn.one_hot(tgt, E, dtype=logits.dtype) * LANG_BIAS
        bias = jnp.where(valid[:, None], bias, 0.0)
        logits = logits + bias[:, None, :]
        topw, topi = jax.lax.top_k(logits, TOP_K)
        weights = jax.nn.softmax(topw, axis=-1)
        gates = jnp.sum(jax.nn.one_hot(topi, E, dtype=weights.dtype) * weights[..., None], axis=-2)
        gates = gates.astype(x.dtype)
        h = jnp.einsum('btd,erd->bter', x, A)
        lora_out = jnp.einsum('bter,bte,eor->bto', h, gates, B)
        return base + SCALING * lora_out

    def _L0_ffn_ref(x, qweight_gu, qzeros_gu, scales_gu, g_idx_gu, qweight_down, qzeros_down, scales_down, g_idx_down):
        import jax, jax.numpy as jnp
        import numpy as np
        HIDDEN = 512
        INTER = 1376
        GROUP = 128
        B, S = (4, 256)
        NIB = jnp.uint32(15)

        def _pack_rows(nib):
            r = nib.reshape(-1, 8, nib.shape[-1])
            shifts = (jnp.arange(8, dtype=jnp.uint32) * 4)[None, :, None]
            return jnp.sum(r << shifts, axis=1, dtype=jnp.uint32)

        def _pack_cols(nib):
            r = nib.reshape(nib.shape[0], -1, 8)
            shifts = (jnp.arange(8, dtype=jnp.uint32) * 4)[None, None, :]
            return jnp.sum(r << shifts, axis=2, dtype=jnp.uint32)

        def _dequant(qw, qz, sc, g_idx):
            shifts = jnp.arange(8, dtype=jnp.uint32) * 4
            wq = qw[:, None, :] >> shifts[None, :, None] & NIB
            wq = wq.reshape(-1, qw.shape[1]).astype(jnp.float32)
            zq = qz[:, :, None] >> shifts[None, None, :] & NIB
            zq = zq.reshape(qz.shape[0], -1).astype(jnp.float32) + 1.0
            return sc[g_idx] * (wq - zq[g_idx])
        w_gu = _dequant(qweight_gu, qzeros_gu, scales_gu, g_idx_gu)
        inter = jnp.einsum('bsh,hf->bsf', x, w_gu)
        gate, up = (inter[..., :INTER], inter[..., INTER:])
        h = jax.nn.silu(gate) * up
        w_d = _dequant(qweight_down, qzeros_down, scales_down, g_idx_down)
        return jnp.einsum('bsf,fh->bsh', h, w_d)

    def _L1_cond_ref(x, weight, adapter_ids):
        import jax, jax.numpy as jnp
        import numpy as np
        MAX_LORAS, OUT, IN = (8, 512, 512)
        B, S = (4, 256)
        w = weight[adapter_ids]
        return jnp.einsum('bsi,boi->bso', x, w)

    def _L1_ffn_ref(x, ln_w, gate_w, up_w, down_w):
        import jax, jax.numpy as jnp
        import numpy as np
        RMS_EPS = 1e-05
        var = jnp.mean(jnp.square(x), axis=-1, keepdims=True)
        nx = x * jax.lax.rsqrt(var + RMS_EPS) * ln_w
        g = jnp.einsum('bsh,ih->bsi', nx, gate_w)
        u = jnp.einsum('bsh,ih->bsi', nx, up_w)
        return jnp.einsum('bsi,hi->bsh', jax.nn.silu(g) * u, down_w)
    x = x + _L0_ffn_ref(_L0_cond_ref(x, itok_B_0_7, L0_cond_W, L0_cond_Wr, L0_cond_A, L0_cond_B), L0_ffn_qweight_gu, L0_ffn_qzeros_gu, L0_ffn_scales_gu, L0_ffn_g_idx_gu, L0_ffn_qweight_down, L0_ffn_qzeros_down, L0_ffn_scales_down, L0_ffn_g_idx_down)
    x = x + _L1_ffn_ref(_L1_cond_ref(x, L1_cond_weight, itok_B_3_7), L1_ffn_ln_w, L1_ffn_gate_w, L1_ffn_up_w, L1_ffn_down_w)
    return x

_drawn_inputs = setup_inputs


def setup_inputs(seed=0):
    import zlib

    import numpy as np

    out = dict(_drawn_inputs(seed))
    spreads = {'L1_ffn_ln_w': (1.0, 0.6)}
    factors = {'L0_cond_Wr': 2.726,
     'L1_cond_weight': 4.523,
     'L1_ffn_gate_w': 4.633,
     'L1_ffn_up_w': 4.52,
     'L1_ffn_down_w': 4.529}
    for name, (base, spread) in spreads.items():
        noise = np.random.default_rng([zlib.crc32(name.encode()), seed]).standard_normal(out[name].shape)
        drawn = base * np.exp(spread * noise) if base else spread * noise
        out[name] = jnp.asarray(drawn.astype(out[name].dtype))
    for name, factor in factors.items():
        out[name] = (out[name] * factor).astype(out[name].dtype)
    return out
```

```python
from contextlib import ExitStack

import concourse.bass as bass
import numpy as np
from concourse import mybir

F32 = mybir.dt.float32
F32R = mybir.dt.float32r
BF16 = mybir.dt.bfloat16
I32 = mybir.dt.int32
U32 = mybir.dt.uint32
U8 = mybir.dt.uint8
ALU = mybir.AluOpType
ACT = mybir.ActivationFunctionType
AX = mybir.AxisListType

P = 128
NBATCH, SEQ, D = 8, 128, 512
T = NBATCH * SEQ
HALF = 512
NH = T // HALF
KD = D // P
E, R = 8, 16
LANG_BIAS, SCALING = 5.0, 2.0
GROUP = 128
F0 = 1376
FT0 = -(-F0 // P)
G_GU, G_DN = D // GROUP, F0 // GROUP
F1 = 1792
FT1 = F1 // P
CH0 = (6, 5)
CH1 = (7, 7)
EPS = 1e-5
YT = 11
C_ID, C_IOTA, C_OGU, C_ODN, C_END = 0, 128, 136, 136 + 44, 136 + 44 + 44


def need(eng, sem, value):
    if not isinstance(value, int) or value > 0:
        eng.wait_ge(sem, value)


def halves(ap):
    return ap.rearrange("p (h t) -> p h t", h=NH)


def build(nc, a, out):
    with ExitStack() as ctx:
        def sb(name, shape, dt):
            return ctx.enter_context(nc.sbuf_tensor(name, shape, dt))

        def sem(name):
            return ctx.enter_context(nc.semaphore(name))

        act_hi = sb("act_hi", [P, KD, T], F32R)
        act_lo = sb("act_lo", [P, KD, T], F32R)
        h_hi = sb("h_hi", [P, YT + 4, T], F32R)
        h_lo = sb("h_lo", [P, YT + 4, T], F32R)
        ring_hi = sb("ring_hi", [P, 2, 1024], F32R)
        ring_lo = sb("ring_lo", [P, 2, 1024], F32R)
        raw = sb("raw", [P, 2, 1024], F32)
        sil = sb("sil", [P, 2, 1024], F32)
        res = sb("res", [P, KD, T], F32)
        cst = sb("cst", [P, C_END], F32)
        shifts = sb("shifts", [P, 2], U32)
        sh8 = shifts[:, 0:1].bitcast(U8)[:, 0:1]
        sh32 = shifts[:, 1:2]
        gidx = sb("gidx", [P, KD + FT0], I32)
        idx_gu = sb("idx_gu", [P, FT0, KD], I32)
        idx_dn = sb("idx_dn", [P, KD, FT0], I32)
        idx_cur = sb("idx_cur", [P, 2, 8], I32)
        zdp = sb("zdp", [P, FT0, D // 8], U32)
        z_dn = sb("z_dn", [P, CH0[0] * P], U8)
        n_dn = sb("n_dn", [P, CH0[0] * P], BF16)
        ids = sb("ids", [P, NBATCH], I32)
        aid = sb("aid", [1, 3 * NBATCH], I32)
        aidf = sb("aidf", [1, 2 * NBATCH], F32)
        lnw = sb("lnw", [P, KD], F32)
        col = sb("col", [P, 8], F32)
        wr = sb("wr", [P, KD, E], F32)

        ident = cst[:, C_ID:C_ID + P]
        res_w = res[:, :, :].rearrange("p k t -> p (k t)")
        ZW = FT0 * 16
        zgp = res_w[:, 0:KD * 2 * ZW].bitcast(U32)
        at = KD * 2 * ZW
        nib_gu = res_w[:, at:at + 256].bitcast(U8)
        z_gu = res_w[:, at + 256:at + 512].bitcast(U8)
        n_gu = res_w[:, at + 512:at + 1024].bitcast(BF16)
        qw = [res_w[:, at + 1024 + 256 * s:at + 1280 + 256 * s].bitcast(U32) for s in range(2)]
        raw_w = raw[:, :, :].rearrange("p s n -> p (s n)")
        w0_hi, w0_lo = (t[:, 0:2, :].rearrange("p a (b n) -> p (a b) n", n=D) for t in (h_hi, h_lo))
        a_hi, a_lo = (t[:, 2, 0:512].rearrange("p (k n) -> p k n", n=P) for t in (h_hi, h_lo))
        b_hi, b_lo = (t[:, 2, 512:1024] for t in (h_hi, h_lo))
        hg_hi, hg_lo = (t[:, 3, :] for t in (h_hi, h_lo))
        ab_raw = sil[:, 0, :]
        hg_full = sil[:, 0, :]
        g_exp = raw[:, 0, :]
        g_T = raw[:, 1, :]
        gt = sil[:, 1, :]
        L_log, L_mx, L_eq, L_g1, L_g2 = (gt[:, 64 * i:64 * i + 64] for i in range(5))
        L_mi = gt[:, 320:384].bitcast(U32)
        L_mif, L_idf, L_w = gt[:, 384:448], gt[:, 448:456], gt[:, 456:512]
        idxf = gt[:, 512:640]

        ps = ctx.enter_context(nc.psum_tensor("ps", [P, 8, HALF], F32))

        s_x = [sem(f"s_x{k}") for k in range(KD)]
        s_wr, s_w0, s_ab, s_cst, s_sh, s_gi, s_id, s_aid, s_ln = (
            sem(n) for n in ("s_wr", "s_w0", "s_ab", "s_cst", "s_sh", "s_gi", "s_id", "s_aid", "s_ln"))
        s_xhi, s_xlo, s_whi0, s_wlo0 = (sem(n) for n in ("s_xhi", "s_xlo", "s_whi0", "s_wlo0"))
        s_log, s_hA, s_gate_c, s_exp, s_gex, s_gTp, s_gT, s_hg, s_hghi, s_hglo = (
            sem(n) for n in ("s_log", "s_hA", "s_gate_c", "s_exp", "s_gex", "s_gTp", "s_gT", "s_hg", "s_hghi", "s_hglo"))
        s_y, s_yhi, s_ylo = (sem(n) for n in ("s_y", "s_yhi", "s_ylo"))
        s_idx, s_idc, s_zg, s_zd, s_aok = (sem(n) for n in ("s_idx", "s_idc", "s_zg", "s_zd", "s_aok"))
        s_v = sem("s_v")
        s_raw = {p: [sem(f"s_raw_{p}{s}") for s in range(2)] for p in ("gu0", "d0", "c", "gu1", "d1")}
        s_qw = {p: [sem(f"s_qw_{p}{s}") for s in range(2)] for p in ("gu0", "d0")}
        s_nib, s_zl, s_zh, s_n, s_wf = (sem(n) for n in ("s_nib", "s_zl", "s_zh", "s_n", "s_wf"))
        s_whi = sem("s_whi")
        s_wlo = sem("s_wlo")
        s_gate = sem("s_gate")
        s_ring = sem("s_ring")
        s_silu, s_hm, s_hhi, s_hlo = (sem(n) for n in ("s_silu", "s_hm", "s_hhi", "s_hlo"))
        s_res = sem("s_res")
        s_xr = sem("s_xr")
        s_rhi, s_rlo, s_sq, s_rc, s_rs, s_zs, s_zt, s_nx, s_nhi, s_nlo, s_vv = (
            sem(n) for n in ("s_rhi", "s_rlo", "s_sq", "s_rc", "s_rs", "s_zs", "s_zt", "s_nx", "s_nhi", "s_nlo", "s_vv"))
        s_out = sem("s_out")

        Q = {"gu0": 0, "d0": FT0, "c": FT0 + 8, "gu1": FT0 + 8 + 2 * NBATCH, "d1": FT0 + 8 + 2 * NBATCH + FT1}
        N = {"gu0": 0, "d0": FT0, "c": FT0 + 8, "gu1": FT0 + 8 + NBATCH, "d1": FT0 + 8 + NBATCH + FT1}
        odd = 1

        def raw_free(eng, q):
            need(eng, s_whi, q - 1)
            need(eng, s_wlo, q - 1)

        block = ctx.enter_context(nc.Block())

        @block.sync
        def _(sp):
            sp.dma_start(wr[:, :, :], a["wrT"]).then_inc(s_wr, 16)
            for k in range(KD):
                sp.dma_start(res[:, k, :], a["xT"][:, k, :]).then_inc(s_x[k], 16)
            sp.dma_start(ab_raw[:, 0:512], a["aT"]).then_inc(s_ab, 16)
            sp.dma_start(raw_w, a["w0T"]).then_inc(s_w0, 16)
            sp.dma_start(ab_raw[:, 512:1024], a["bT"]).then_inc(s_ab, 16)

            def load_qw(i, s, half_pair):
                for hp in range(2):
                    sp.dma_start(qw[s][64 * hp:64 * hp + 64, :], a["qw_gu"][bass.ds(i, 1), :, :].rearrange("o r c -> (o r) c")
                                 ).then_inc(s_qw["gu0"][s], 16)

            sp.wait_ge(s_xlo, KD)
            sp.wait_ge(s_xhi, KD)
            sp.wait_ge(s_log, 1)
            for i in range(2):
                load_qw(i, i, 0)
            with sp.Fori(0, (FT0 - 3) // 2) as j:
                for s in range(2):
                    need(sp, s_nib, 2 * j + s + 1)
                    load_qw(2 * j + s + 2, s, 0)
            need(sp, s_nib, FT0 - 2)
            load_qw(FT0 - 1, (FT0 - 1) % 2, 0)

            def load_qd(m, c):
                k0, cnt = CH0[0] * c, CH0[c]
                sp.dma_start(sil[:, 1 - c, 0:cnt * P].bitcast(U32).rearrange("p (k n) -> p k n", n=P),
                             a["qw_dn"][:, bass.ds(m, 1), k0:k0 + cnt, :].rearrange("p o k n -> p (o k) n")
                             ).then_inc(s_qw["d0"][c], 16)

            need(sp, s_hlo, FT0 - 1)
            load_qd(0, 0)
            need(sp, s_hlo, FT0)
            load_qd(0, 1)
            need(sp, s_hhi, FT0)
            sp.dma_start(res[:, :, :], a["xT"]).then_inc(s_xr, 16)
            with sp.Fori(1, KD) as m:
                for c in range(2):
                    need(sp, s_wf, FT0 + 2 * m + c - 1)
                    load_qd(m, c)

            sp.wait_ge(s_aok, 1)

            def load_adapter(b, c):
                ident_b = sp.value_load(aid[0:1, bass.ds(b + 2 * NBATCH, 1)], min_val=0, max_val=NBATCH - 1)
                raw_free(sp, 2 * b + c + Q["c"])
                sp.dma_start(raw[:, 1 - c, :], a["w1T"][bass.ds(ident_b, 1), :, 1024 * c:1024 * c + 1024].rearrange(
                    "o p n -> (o p) n")).then_inc(s_raw["c"][c], 16)

            with sp.Fori(0, NBATCH) as b:
                for c in range(2):
                    load_adapter(b, c)

            with sp.Fori(0, FT1 // 2) as j:
                for s in range(2):
                    raw_free(sp, 2 * j + s + Q["gu1"])
                    sp.dma_start(raw[:, 1 - s, :], a["gu1"][bass.ds(2 * j + s, 1), :, :].rearrange("o p n -> (o p) n")
                                 ).then_inc(s_raw["gu1"][s], 16)
            with sp.Fori(0, KD) as m:
                for c in range(2):
                    n = CH1[c] * P
                    raw_free(sp, 2 * m + c + Q["d1"])
                    sp.dma_start(raw[:, 1 - c, 0:n], a["d1"][bass.ds(m, 1), :, n * c:n * c + n].rearrange("o p n -> (o p) n")
                                 ).then_inc(s_raw["d1"][c], 16)
            with sp.Fori(0, KD) as m:
                sp.wait_ge(s_res, m + KD + 1)
                sp.dma_start(out[bass.ds(m, 1), :, :].rearrange("o p t -> (o p) t"), res[:, bass.ds(m, 1), :].rearrange(
                    "p o t -> p (o t)")).then_inc(s_out, 16)
            sp.wait_ge(s_out, 16 * KD)

        @block.gpsimd
        def _(pool):
            pool.dma_start(cst[:, :], a["cst"]).then_inc(s_cst, 16)
            pool.dma_start(gidx[:, :], a["gidx"]).then_inc(s_gi, 16)
            pool.dma_start(ids[:, :], a["ids"].partition_broadcast(P)).then_inc(s_id, 16)
            pool.dma_start(aid[:, 0:NBATCH], a["aids"].partition_broadcast(1)).then_inc(s_aid, 16)
            pool.dma_start(lnw[:, :], a["lnw"]).then_inc(s_ln, 16)
            pool.dma_start(shifts[:, :], a["shifts"]).then_inc(s_sh, 16)

            def gather(dst, table, index, done):
                pool.indirect_dma_start(dst, None, table, bass.IndirectOffsetOnAxis(ap=index, axis=0)).then_inc(done, 16)

            pool.wait_ge(s_idx, 2)
            for i in range(FT0):
                gather(zdp[:, i, :], a["qz_dn"], idx_dn[:, 0, i:i + 1], s_zd)
            pool.wait_ge(s_xlo, KD)
            pool.wait_ge(s_xhi, KD)
            pool.wait_ge(s_log, 1)
            for k in range(KD):
                gather(zgp[:, 2 * ZW * k:2 * ZW * (k + 1)], a["qz_gu"], idx_gu[:, 0, k:k + 1], s_zg)

            def scales_gu(i, s):
                raw_free(pool, i)
                pool.tensor_copy(idx_cur[:, s, 0:KD], idx_gu[:, bass.ds(i, 1), :].rearrange("p o k -> p (o k)")).then_inc(s_idc, 1)
                pool.drain()
                for k in range(KD):
                    gather(raw[:, s, 256 * k:256 * k + 256], a["sc_gu"], idx_cur[:, s, k:k + 1], s_raw["gu0"][s])

            pool.wait_ge(s_gT, 1)
            pool.wait_ge(s_gTp, 1)
            pool.wait_ge(s_hg, 1)
            for i in range(2):
                scales_gu(i, i)
            with pool.Fori(1, FT0 // 2) as j:
                for s in range(2):
                    scales_gu(2 * j + s, s)
            scales_gu(FT0 - 1, 0)

            with pool.Fori(0, KD) as m:
                for c in range(2):
                    k0, cnt = CH0[0] * c, CH0[c]
                    raw_free(pool, 2 * m + c + Q["d0"])
                    pool.tensor_copy(idx_cur[:, 1 - c, 0:cnt], idx_dn[:, bass.ds(m, 1), k0:k0 + cnt].rearrange("p o k -> p (o k)")
                                     ).then_inc(s_idc, 1)
                    pool.drain()
                    for k in range(cnt):
                        gather(raw[:, 1 - c, P * k:P * k + P], a["sc_dn"], idx_cur[:, 1 - c, k:k + 1], s_raw["d0"][c])

        @block.scalar
        def _(act):
            def hi(dst, src, done):
                act.activation(dst, src, ACT.Copy).then_inc(done, 1)

            for k in range(KD):
                act.wait_ge(s_x[k], 16)
                hi(act_hi[:, k, :], res[:, k, :], s_xhi)
            act.wait_ge(s_ab, 32)
            hi(h_hi[:, 2, :], ab_raw, s_whi0)
            act.wait_ge(s_w0, 16)
            hi(h_hi[:, 0:2, :], raw[:, :, :], s_whi0)
            act.wait_ge(s_gate_c, 1)
            act.activation(L_w[:, 8:16], L_w[:, 0:8], ACT.Exp).then_inc(s_exp, 1)
            act.wait_ge(s_gTp, 1)
            act.activation(halves(g_T), ps[:, 2:4, :], ACT.Copy).then_inc(s_gT, 1)
            act.wait_ge(s_hg, 1)
            hi(hg_hi, hg_full, s_hghi)
            for m, b in enumerate((0, 4, 6, 2)):
                act.wait_ge(s_y, m + 1)
                hi(halves(h_hi[:, YT + m, :]), ps[:, b:b + 2, :], s_yhi)

            def w_hi(q, n, s, width, loaded, value):
                need(act, loaded, value)
                need(act, s_ring, n - 1)
                hi(ring_hi[:, s, 0:width], raw[:, s, 0:width], s_whi)

            def w_hi_gu(ph, i, s):
                if ph == "gu0":
                    w_hi(i, i, s, 1024, s_wf, i + 1)
                else:
                    w_hi(i + Q[ph], i + N[ph], 1 - s, 1024, s_raw[ph][s], (i - s) * 8 + 16)

            def w_hi_dn(ph, m, c):
                if ph == "d0":
                    w_hi(2 * m + c + Q[ph], 2 * m + c + N[ph], 1 - c, CH0[c] * P, s_wf, FT0 + 2 * m + c + 1)
                else:
                    w_hi(2 * m + c + Q[ph], 2 * m + c + N[ph], 1 - c, CH1[c] * P, s_raw[ph][c], 16 * m + 16)

            def silu(i, s, base):
                need(act, s_gate, i + base + 1)
                need(act, s_hlo, i + base - 1)
                act.activation(halves(sil[:, s, :]), ps[:, 4 * s:4 * s + 2, :], ACT.Silu).then_inc(s_silu, 1)

            def h_split(i, s, base):
                need(act, s_hm, i + base + 1)
                hi(h_hi[:, bass.ds(i, 1), :].rearrange("p o t -> p (o t)"), sil[:, s, :], s_hhi)

            def gu_step(ph, i, s, base, then):
                then()
                silu(i, s, base)
                h_split(i, s, base)

            w_hi_gu("gu0", 0, 0)
            for i in range(2):
                gu_step("gu0", i, i, 0, lambda: w_hi_gu("gu0", i + 1, 1 - i))
            with act.Fori(1, FT0 // 2) as j:
                for s in range(2):
                    i = 2 * j + s
                    gu_step("gu0", i, s, 0, lambda: w_hi_gu("gu0", i + 1, 1 - s))
            gu_step("gu0", FT0 - 1, 0, 0, lambda: w_hi_dn("d0", 0, 0))

            w_hi_dn("d0", 0, 1)
            with act.Fori(1, KD) as m:
                for c in range(2):
                    w_hi_dn("d0", m, c)

            def batch_a(b, s):
                for c in range(2):
                    need(act, s_raw["c"][c], 16 * b + 16)
                    need(act, s_ring, b + N["c"] - 1)
                    hi(h_hi[:, YT + 2 * s + c, :], raw[:, 1 - c, :], s_whi)

            def batch_z(b, s):
                need(act, s_ring, b + N["c"] + 1)
                need(act, s_zt, b - 1)
                act.activation(sil[:, s, 0:D], ps[:, 4 + s, :], ACT.Square, accum_out=col[:, s:s + 1]).then_inc(s_sq, 1)

            def batch_n(b, s):
                need(act, s_nx, b + 1)
                hi(act_hi[:, :, bass.ds(b * SEQ, SEQ)], sil[:, s, D:2 * D].rearrange("p (k t) -> p k t", k=KD), s_nhi)

            def batch_r(b, s):
                need(act, s_rc, b + 1)
                act.activation(col[:, 4 + s:5 + s], col[:, 2 + s:3 + s], ACT.Sqrt).then_inc(s_rs, 1)

            batch_a(0, 0)
            for b in range(2):
                batch_a(b + 1, 1 - b)
                batch_z(b, b)
                if b:
                    batch_n(0, 0)
                batch_r(b, b)
            with act.Fori(1, NBATCH // 2 - 1) as j:
                for s in range(2):
                    b = 2 * j + s
                    batch_a(b + 1, 1 - s)
                    batch_z(b, s)
                    batch_n(b - 1, 1 - s)
                    batch_r(b, s)
            for b in range(NBATCH - 2, NBATCH):
                if b == NBATCH - 2:
                    batch_a(b + 1, 1)
                batch_z(b, b % 2)
                batch_n(b - 1, 1 - b % 2)
                batch_r(b, b % 2)
            w_hi_gu("gu1", 0, 0)
            batch_n(NBATCH - 1, 1)

            for i in range(2):
                gu_step("gu1", i, i, FT0, lambda: w_hi_gu("gu1", i + 1, 1 - i))
            with act.Fori(1, FT1 // 2 - 1) as j:
                for s in range(2):
                    i = 2 * j + s
                    gu_step("gu1", i, s, FT0, lambda: w_hi_gu("gu1", i + 1, 1 - s))
            gu_step("gu1", FT1 - 2, 0, FT0, lambda: w_hi_gu("gu1", FT1 - 1, 1))
            gu_step("gu1", FT1 - 1, 1, FT0, lambda: w_hi_dn("d1", 0, 0))
            w_hi_dn("d1", 0, 1)
            with act.Fori(1, KD) as m:
                for c in range(2):
                    w_hi_dn("d1", m, c)

        @block.vector
        def _(dve):
            done = [0]

            def own(ins):
                done[0] += 1
                ins.then_inc(s_v, 1)
                dve.wait_ge(s_v, done[0])

            def lo(dst, src, hi_part, done_sem):
                dve.tensor_tensor(dst, src, hi_part.bitcast(F32), ALU.subtract).then_inc(done_sem, 1)

            dve.wait_ge(s_gi, 16)
            dve.wait_ge(s_cst, 16)
            g_f, g_n = idxf[:, 0:15], idxf[:, 16:31]
            own(dve.tensor_copy(g_f, gidx[:, :]))
            for lo_c, hi_c, n in ((0, KD, G_GU), (KD, KD + FT0, G_DN)):
                own(dve.tensor_scalar(g_n[:, lo_c:hi_c], g_f[:, lo_c:hi_c], 0.0, float(n), ALU.is_lt, ALU.mult))
                own(dve.tensor_tensor(g_n[:, lo_c:hi_c], g_f[:, lo_c:hi_c], g_n[:, lo_c:hi_c], ALU.add))
                own(dve.tensor_scalar(g_n[:, lo_c:hi_c], g_n[:, lo_c:hi_c], 0.0, float(n - 1), ALU.max, ALU.min))
            dve.tensor_tensor(idx_gu[:, :, :], g_n[:, 0:KD].unsqueeze(1).to_broadcast([P, FT0, KD]),
                              cst[:, C_OGU:C_ODN].rearrange("p (i k) -> p i k", k=KD), ALU.add).then_inc(s_idx, 1)
            dve.tensor_tensor(idx_dn[:, :, :], g_n[:, KD:KD + FT0].unsqueeze(1).to_broadcast([P, KD, FT0]),
                              cst[:, C_ODN:C_END].rearrange("p (m i) -> p m i", i=FT0), ALU.add).then_inc(s_idx, 1)
            dve.wait_ge(s_aid, 16)
            a_f, a_n = aidf[:, 0:NBATCH], aidf[:, NBATCH:2 * NBATCH]
            own(dve.tensor_copy(a_f, aid[:, 0:NBATCH]))
            own(dve.tensor_scalar(a_n, a_f, 0.0, float(NBATCH), ALU.is_lt, ALU.mult))
            own(dve.tensor_tensor(a_n, a_f, a_n, ALU.add))
            dve.tensor_scalar(aid[:, 2 * NBATCH:3 * NBATCH], a_n, 0.0, float(NBATCH - 1), ALU.max, ALU.min).then_inc(s_aok, 1)

            for k in range(KD):
                dve.wait_ge(s_xhi, k + 1)
                lo(act_lo[:, k, :], res[:, k, :], act_hi[:, k, :], s_xlo)
            dve.wait_ge(s_whi0, 1)
            lo(h_lo[:, 2, :], ab_raw, h_hi[:, 2, :], s_wlo0)

            def g3(ap):
                return ap.rearrange("p (b e) -> p b e", e=E)

            iota = cst[:, C_IOTA:C_IOTA + E].unsqueeze(1).to_broadcast([P, NBATCH, E])

            def per_batch(ap):
                return ap.unsqueeze(2).to_broadcast([P, NBATCH, E])

            dve.wait_ge(s_id, 16)
            own(dve.tensor_copy(L_idf, ids[:, :]))
            own(dve.tensor_tensor(g3(L_eq), per_batch(L_idf), iota, ALU.is_equal))
            dve.wait_ge(s_log, 1)
            own(dve.scalar_tensor_tensor(out=L_log, in0=L_eq, scalar=LANG_BIAS, in1=ps[:, 2, 0:64],
                                         op0=ALU.mult, op1=ALU.add))
            for b in range(NBATCH):
                ins = dve.max(L_mx[:, 8 * b:8 * b + 8], L_log[:, 8 * b:8 * b + 8])
            own(ins)
            for b in range(NBATCH):
                ins = dve.max_index(L_mi[:, 8 * b:8 * b + 8], L_mx[:, 8 * b:8 * b + 8], L_log[:, 8 * b:8 * b + 8])
            own(ins)
            dve.tensor_tensor(L_w[:, 0:8], g3(L_mx)[:, :, 1], g3(L_mx)[:, :, 0], ALU.subtract).then_inc(s_gate_c, 1)
            own(dve.tensor_copy(L_mif, L_mi))
            own(dve.tensor_tensor(g3(L_g1), per_batch(g3(L_mif)[:, :, 0]), iota, ALU.is_equal))
            own(dve.tensor_tensor(g3(L_g2), per_batch(g3(L_mif)[:, :, 1]), iota, ALU.is_equal))
            dve.wait_ge(s_exp, 1)
            own(dve.tensor_scalar(L_w[:, 16:24], L_w[:, 8:16], 1.0, None, ALU.add))
            own(dve.reciprocal(L_w[:, 24:32], L_w[:, 16:24]))
            own(dve.tensor_scalar(L_w[:, 32:40], L_w[:, 24:32], SCALING, None, ALU.mult))
            own(dve.tensor_tensor(L_w[:, 40:48], L_w[:, 32:40], L_w[:, 8:16], ALU.mult))
            own(dve.tensor_tensor(g3(L_g1), g3(L_g1), per_batch(L_w[:, 32:40]), ALU.mult))
            own(dve.tensor_tensor(g3(L_g2), g3(L_g2), per_batch(L_w[:, 40:48]), ALU.mult))
            own(dve.tensor_tensor(L_g1, L_g1, L_g2, ALU.add))
            dve.wait_ge(s_whi0, 2)
            own(dve.tensor_tensor(h_lo[:, 0:2, :], raw[:, :, :], h_hi[:, 0:2, :].bitcast(F32), ALU.subtract))
            dve.tensor_copy(g_exp.rearrange("p (g r) -> p g r", r=R),
                            L_g1.unsqueeze(2).to_broadcast([P, NBATCH * E, R])).then_inc(s_gex, 1)
            dve.wait_ge(s_gT, 1)
            dve.wait_ge(s_hA, 1)
            dve.tensor_tensor(halves(hg_full), ps[:, 6:8, :], halves(g_T), ALU.mult).then_inc(s_hg, 1)
            dve.wait_ge(s_hghi, 1)
            lo(hg_lo, hg_full, hg_hi, s_hglo)
            for m, b in enumerate((0, 4, 6, 2)):
                dve.wait_ge(s_yhi, m + 1)
                lo(halves(h_lo[:, YT + m, :]), ps[:, b:b + 2, :], halves(h_hi[:, YT + m, :]), s_ylo)

            def w_lo(q, s, width):
                need(dve, s_whi, q + 1)
                lo(ring_lo[:, s, 0:width], raw[:, s, 0:width], ring_hi[:, s, 0:width], s_wlo)

            dve.wait_ge(s_sh, 16)
            dve.wait_ge(s_zg, 16 * KD)
            zg8 = zgp.bitcast(U8).rearrange("p (g w) -> p g w", g=2 * KD)
            z3 = z_gu.rearrange("p (g w e) -> p g w e", g=2 * KD, e=2)

            def dequant_gu(i, s):
                need(dve, s_qw["gu0"][s], (i - s) * 16 + 32)
                need(dve, s_n, i)
                words = qw[s].bitcast(U8).rearrange("p (c j) -> p j c", j=4)
                dve.tensor_scalar(nib_gu.rearrange("p (j c) -> p j c", j=4), words, sh8, 15,
                                  ALU.logical_shift_right, ALU.bitwise_and).then_inc(s_nib, 1)
                zw = zg8[:, :, bass.ds(i * 64, 64)]
                dve.tensor_scalar(z3[:, :, :, 0], zw, 15, None, ALU.bitwise_and).then_inc(s_zl, 1)
                dve.tensor_scalar(z3[:, :, :, 1], zw, 4, None, ALU.logical_shift_right).then_inc(s_zh, 1)
                need(dve, s_nib, i + 1)
                need(dve, s_zl, i + 1)
                need(dve, s_zh, i + 1)
                need(dve, s_wf, i)
                dve.scalar_tensor_tensor(out=n_gu, in0=nib_gu, scalar=1.0, in1=z_gu, op0=ALU.subtract,
                                         op1=ALU.subtract).then_inc(s_n, 1)
                need(dve, s_n, i + 1)
                need(dve, s_raw["gu0"][s], (i - s) * 32 + 64)
                dve.tensor_tensor(raw[:, s, :], raw[:, s, :], n_gu, ALU.mult).then_inc(s_wf, 1)

            def dequant_dn(m, c):
                k0, cnt = CH0[0] * c, CH0[c]
                e = 2 * m + c + FT0
                need(dve, s_qw["d0"][c], 16 * m + 16)
                q = sil[:, 1 - c, 0:cnt * P].bitcast(U32)
                dve.tensor_scalar(q, q, sh32, 15, ALU.logical_shift_right, ALU.bitwise_and).then_inc(s_nib, 1)
                zw = zdp[:, k0:k0 + cnt, :].bitcast(U8)[:, :, bass.ds(m * 64, 64)]
                z4 = z_dn[:, 0:cnt * P].rearrange("p (k w e) -> p k w e", k=cnt, e=2)
                need(dve, s_n, e)
                dve.tensor_scalar(z4[:, :, :, 0], zw, 15, None, ALU.bitwise_and).then_inc(s_zl, 1)
                dve.tensor_scalar(z4[:, :, :, 1], zw, 4, None, ALU.logical_shift_right).then_inc(s_zh, 1)
                need(dve, s_nib, e + 1)
                need(dve, s_zl, e + 1)
                need(dve, s_zh, e + 1)
                need(dve, s_wf, e)
                dve.scalar_tensor_tensor(out=n_dn[:, 0:cnt * P], in0=q, scalar=1.0, in1=z_dn[:, 0:cnt * P],
                                         op0=ALU.subtract, op1=ALU.subtract).then_inc(s_n, 1)
                need(dve, s_n, e + 1)
                need(dve, s_raw["d0"][c], (m + 1) * (16 * cnt))
                dve.tensor_tensor(raw[:, 1 - c, 0:cnt * P], raw[:, 1 - c, 0:cnt * P], n_dn[:, 0:cnt * P],
                                  ALU.mult).then_inc(s_wf, 1)

            def h_step(i, s, base, nbase):
                need(dve, s_silu, i + base + 1)
                need(dve, s_ring, i + nbase + 1)
                dve.tensor_tensor(halves(sil[:, s, :]), halves(sil[:, s, :]), ps[:, 4 * s + 2:4 * s + 4, :],
                                  ALU.mult).then_inc(s_hm, 1)
                need(dve, s_hhi, i + base + 1)
                t = bass.ds(i, 1)
                lo(h_lo[:, t, :].rearrange("p o t -> p (o t)"), sil[:, s, :],
                   h_hi[:, t, :].rearrange("p o t -> p (o t)"), s_hlo)

            dequant_gu(0, 0)
            w_lo(0, 0, 1024)
            for i in range(2):
                dequant_gu(i + 1, 1 - i)
                w_lo(i + 1, 1 - i, 1024)
                h_step(i, i, 0, N["gu0"])
            with dve.Fori(1, FT0 // 2) as j:
                for s in range(2):
                    i = 2 * j + s
                    dequant_gu(i + 1, 1 - s)
                    w_lo(i + 1, 1 - s, 1024)
                    h_step(i, s, 0, N["gu0"])
            dve.wait_ge(s_zd, 16 * FT0)
            dequant_dn(0, 0)
            w_lo(Q["d0"], 1, CH0[0] * P)
            h_step(FT0 - 1, 0, 0, N["gu0"])

            def down_chunk0(m, c):
                dequant_dn(m, c)
                w_lo(2 * m + c + Q["d0"], 1 - c, CH0[c] * P)

            def add_res(m, bank, n_last, base):
                need(dve, s_ring, n_last + 1)
                t = res[:, bass.ds(m, 1), :].rearrange("p o (h t) -> p (o h) t", h=NH)
                dve.tensor_tensor(t, ps[:, bank, :], t, ALU.add).then_inc(s_res, 1)

            down_chunk0(0, 1)
            dve.wait_ge(s_xr, 16)
            for m in range(KD):
                if m < KD - 1:
                    for c in range(2):
                        down_chunk0(m + 1, c)
                add_res(m, slice((4 + 2 * m) % 8, (4 + 2 * m) % 8 + 2), N["d0"] + 2 * m + 1, 0)

            def split_r(b, s):
                for c in range(2):
                    need(dve, s_whi, 2 * b + c + Q["c"] + 1)
                    lo(h_lo[:, YT + 2 * s + c, :], raw[:, 1 - c, :], h_hi[:, YT + 2 * s + c, :], s_wlo)
                r = res[:, :, bass.ds(b * SEQ, SEQ)]
                r_hi, r_lo = (t[:, 1 - s, 0:D].rearrange("p (k t) -> p k t", k=KD) for t in (ring_hi, ring_lo))
                need(dve, s_ring, b + N["c"] - 1)
                dve.tensor_copy(r_hi, r).then_inc(s_rhi, 1)
                need(dve, s_rhi, b + 1)
                lo(r_lo, r, r_hi, s_rlo)

            def var(b, s):
                need(dve, s_sq, b + 1)
                dve.tensor_scalar(col[:, 6 + s:7 + s], col[:, s:s + 1], 1.0 / D, EPS, ALU.mult, ALU.add).then_inc(s_vv, 1)
                need(dve, s_vv, b + 1)
                dve.reciprocal(col[:, 2 + s:3 + s], col[:, 6 + s:7 + s]).then_inc(s_rc, 1)

            def norm(b, s):
                need(dve, s_rs, b + 1)
                dve.tensor_scalar(sil[:, s, 0:D], ps[:, 4 + s, :], col[:, 4 + s:5 + s], None, ALU.mult).then_inc(s_zs, 1)

            def weigh(b, s):
                need(dve, s_zt, b + 1)
                need(dve, s_nlo, b - 1)
                nx = sil[:, s, D:2 * D].rearrange("p (k t) -> p k t", k=KD)
                dve.tensor_tensor(nx, ps[:, 6 + s, :].rearrange("p (k t) -> p k t", k=KD),
                                  lnw[:, :].unsqueeze(2).to_broadcast([P, KD, SEQ]), ALU.mult).then_inc(s_nx, 1)
                need(dve, s_nhi, b + 1)
                t = bass.ds(b * SEQ, SEQ)
                lo(act_lo[:, :, t], nx, act_hi[:, :, t], s_nlo)

            dve.wait_ge(s_ln, 16)
            dve.wait_ge(s_res, KD)
            split_r(0, 0)
            for b in range(2):
                split_r(b + 1, 1 - b)
                var(b, b)
                if b:
                    weigh(0, 0)
                norm(b, b)
            with dve.Fori(1, NBATCH // 2 - 1) as j:
                for s in range(2):
                    b = 2 * j + s
                    split_r(b + 1, 1 - s)
                    var(b, s)
                    weigh(b - 1, 1 - s)
                    norm(b, s)
            for b in range(NBATCH - 2, NBATCH):
                if b == NBATCH - 2:
                    split_r(b + 1, 1)
                var(b, b % 2)
                weigh(b - 1, 1 - b % 2)
                norm(b, b % 2)
            w_lo(Q["gu1"], 1, 1024)
            weigh(NBATCH - 1, 1)

            def gu1_step(i, s):
                w_lo(i + 1 + Q["gu1"], s, 1024)
                h_step(i, s, FT0, N["gu1"])

            for i in range(2):
                gu1_step(i, i)
            with dve.Fori(1, FT1 // 2 - 1) as j:
                for s in range(2):
                    gu1_step(2 * j + s, s)
            gu1_step(FT1 - 2, 0)
            w_lo(Q["d1"], 1, CH1[0] * P)
            h_step(FT1 - 1, 1, FT0, N["gu1"])
            w_lo(Q["d1"] + 1, 0, CH1[1] * P)
            for m in range(KD):
                if m < KD - 1:
                    for c in range(2):
                        w_lo(2 * (m + 1) + c + Q["d1"], 1 - c, CH1[c] * P)
                add_res(m, slice(2 * m, 2 * m + 2), N["d1"] + 2 * m + 1, KD)

        @block.tensor
        def _(pe):
            def mm3(bank, w_hi, w_lo, v_hi, v_lo, first, last):
                for hf in range(NH):
                    t = slice(HALF * hf, HALF * hf + HALF)
                    pe.matmul(ps[:, bank + hf, :], w_hi, v_hi[:, t], start=first, stop=False)
                    pe.matmul(ps[:, bank + hf, :], w_hi, v_lo[:, t], start=False, stop=False)
                for hf in range(NH):
                    t = slice(HALF * hf, HALF * hf + HALF)
                    ins = pe.matmul(ps[:, bank + hf, :], w_lo, v_hi[:, t], start=False, stop=last)
                return ins

            pe.wait_ge(s_wr, 16)
            for k in range(KD):
                pe.wait_ge(s_x[k], 16)
            for b in range(NBATCH):
                for k in range(KD):
                    ins = pe.matmul(ps[:, 2, E * b:E * b + E], res[:, k, SEQ * b:SEQ * b + SEQ], wr[:, k, :],
                                    start=(k == 0), stop=(k == KD - 1))
            ins.then_inc(s_log, 1)
            pe.wait_ge(s_xhi, KD)
            pe.wait_ge(s_xlo, KD)
            pe.wait_ge(s_wlo0, 1)
            for k in range(KD):
                ins = mm3(6, a_hi[:, k, :], a_lo[:, k, :], act_hi[:, k, :], act_lo[:, k, :], k == 0, k == KD - 1)
            ins.then_inc(s_hA, 1)

            def base(m, bank):
                for k in range(KD):
                    c = slice(P * m, P * m + P)
                    mm3(bank, w0_hi[:, k, c], w0_lo[:, k, c], act_hi[:, k, :], act_lo[:, k, :], k == 0, False)

            def lora(m, bank):
                c = slice(P * m, P * m + P)
                mm3(bank, b_hi[:, c], b_lo[:, c], hg_hi, hg_lo, False, True).then_inc(s_y, 1)

            pe.wait_ge(s_gex, 1)
            base(0, 0)
            base(1, 4)
            pe.wait_ge(s_cst, 16)
            for b in range(NBATCH):
                ins = pe.transpose(ps[:, 2 + b // 4, P * (b % 4):P * (b % 4) + P], g_exp[:, P * b:P * b + P], ident)
            ins.then_inc(s_gTp, 1)
            pe.wait_ge(s_hglo, 1)
            lora(0, 0)
            lora(1, 4)
            base(2, 6)
            lora(2, 6)
            base(3, 2)
            lora(3, 2)

            def weights_ready(q):
                need(pe, s_whi, q + 1)
                need(pe, s_wlo, q + 1)

            def gate_up(q, s, i, slot, act_at):
                weights_ready(q)
                need(pe, s_hm, i - 1)
                for g in range(2):
                    for k in range(KD):
                        c = slice(256 * k + P * g, 256 * k + P * g + P)
                        ins = mm3(4 * s + 2 * g, ring_hi[:, slot, c], ring_lo[:, slot, c],
                                  act_at[0][:, k, :], act_at[1][:, k, :], k == 0, k == KD - 1)
                    ins.then_inc(s_ring if g else s_gate, 1)

            y_at = (h_hi[:, YT:YT + KD, :], h_lo[:, YT:YT + KD, :])
            pe.wait_ge(s_ylo, KD)
            for i in range(2):
                gate_up(i, i, i, i, y_at)
            with pe.Fori(1, FT0 // 2) as j:
                for s in range(2):
                    gate_up(2 * j + s, s, 2 * j + s, s, y_at)
            gate_up(FT0 - 1, 0, FT0 - 1, 0, y_at)

            def down(m, q0, chunks, bank, h_done):
                for c in range(2):
                    weights_ready(q0 + 2 * m + c)
                    for k in range(chunks[c]):
                        i = chunks[0] * c + k
                        if m == 0:
                            pe.wait_ge(s_hhi, h_done + i + 1)
                            pe.wait_ge(s_hlo, h_done + i + 1)
                        w = slice(P * k, P * k + P)
                        ins = mm3(bank, ring_hi[:, 1 - c, w], ring_lo[:, 1 - c, w], h_hi[:, i, :], h_lo[:, i, :],
                                  i == 0, i == sum(chunks) - 1)
                    ins.then_inc(s_ring, 1)

            pe.wait_ge(s_hm, FT0 - 1)
            for m in range(KD):
                down(m, Q["d0"], CH0, (4 + 2 * m) % 8, 0)

            def z_product(b, s):
                need(pe, s_rhi, b + 1)
                need(pe, s_rlo, b + 1)
                need(pe, s_whi, 2 * b + Q["c"] + 2)
                need(pe, s_wlo, 2 * b + Q["c"] + 2)
                need(pe, s_zs, b - 1)
                w_hi, w_lo = (t[:, YT + 2 * s:YT + 2 * s + 2, :].rearrange("p a (c n) -> p (a c) n", n=D)
                              for t in (h_hi, h_lo))
                for k in range(KD):
                    c = slice(SEQ * k, SEQ * k + SEQ)
                    pe.matmul(ps[:, 4 + s, :], ring_hi[:, 1 - s, c], w_hi[:, k, :], start=(k == 0), stop=False)
                    pe.matmul(ps[:, 4 + s, :], ring_hi[:, 1 - s, c], w_lo[:, k, :], start=False, stop=False)
                    ins = pe.matmul(ps[:, 4 + s, :], ring_lo[:, 1 - s, c], w_hi[:, k, :], start=False, stop=(k == KD - 1))
                ins.then_inc(s_ring, 1)

            def turn(b, s):
                need(pe, s_zs, b + 1)
                need(pe, s_nx, b - 1)
                for k in range(KD):
                    ins = pe.transpose(ps[:, 6 + s, P * k:P * k + P], sil[:, s, P * k:P * k + P], ident)
                ins.then_inc(s_zt, 1)

            z_product(0, 0)
            z_product(1, 1)
            turn(0, 0)
            with pe.Fori(1, NBATCH // 2) as j:
                for s in range(2):
                    z_product(2 * j + s, s)
                    turn(2 * j + s - 1, 1 - s)
            turn(NBATCH - 1, 1)

            pe.wait_ge(s_nhi, NBATCH)
            pe.wait_ge(s_nlo, NBATCH)
            z_at = (act_hi, act_lo)
            for i in range(2):
                gate_up(i + Q["gu1"], i, i + FT0, 1 - i, z_at)
            with pe.Fori(1, FT1 // 2) as j:
                for s in range(2):
                    gate_up(2 * j + s + Q["gu1"], s, 2 * j + s + FT0, 1 - s, z_at)
            pe.wait_ge(s_hm, FT0 + FT1 - 1)
            for m in range(KD):
                down(m, Q["d1"], CH1, 2 * m, FT0)


def kernel(**inputs):
    import concourse.bacc as bacc
    from concourse.bass_utils import run_bass_kernel_spmd

    v = {k: np.asarray(x) for k, x in inputs.items()}
    p = np.arange(P)
    k_of = 8 * (p[:, None] % 64) + 2 * np.arange(KD)[None, :] + p[:, None] // 64

    def rows(w):
        return np.ascontiguousarray(w.reshape(-1, P, w.shape[1]).transpose(1, 0, 2).reshape(P, -1))

    def pad_f(w):
        w = w.reshape(*w.shape[:-1], 2, -1)
        width = FT0 * P * w.shape[-1] // F0 if w.shape[-1] == F0 else FT0 * 16
        return np.concatenate([w, np.zeros((*w.shape[:-1], width - w.shape[-1]), w.dtype)], axis=-1)

    order = k_of.T.reshape(-1)
    qg = pad_f(v["L0_ffn_qweight_gu"]).reshape(64, 2, FT0, P)
    sg = pad_f(v["L0_ffn_scales_gu"]).reshape(G_GU, 2, FT0, P)
    qd = np.repeat(v["L0_ffn_qweight_down"], 8, axis=0)
    qd = np.concatenate([qd, np.zeros((FT0 * P - F0, D), qd.dtype)]).reshape(FT0, P, KD, P)
    gd = np.concatenate([v["L0_ffn_g_idx_down"], np.zeros(FT0 * P - F0, v["L0_ffn_g_idx_down"].dtype)])
    gu1 = np.stack([v["L1_ffn_gate_w"].reshape(FT1, P, KD, P), v["L1_ffn_up_w"].reshape(FT1, P, KD, P)])
    cst = np.zeros((P, C_END), np.float32)
    cst[:, C_ID:C_ID + P] = np.eye(P)
    cst[:, C_IOTA:C_IOTA + E] = np.arange(E)
    cst[:, C_OGU:C_ODN] = np.repeat(G_GU * np.arange(FT0), KD)
    cst[:, C_ODN:C_END] = np.repeat(G_DN * np.arange(KD), FT0)
    arrays = {
        "xT": v["x"].reshape(T, KD, P).transpose(2, 1, 0),
        "wrT": rows(v["L0_cond_Wr"].T).reshape(P, KD, E),
        "aT": rows(v["L0_cond_A"].reshape(E * R, D).T),
        "w0T": rows(v["L0_cond_W"].T[:, order]),
        "bT": v["L0_cond_B"].transpose(0, 2, 1).reshape(E * R, D)[:, order],
        "qw_gu": qg.transpose(2, 0, 1, 3).reshape(FT0, 64, 256),
        "sc_gu": sg.transpose(2, 0, 1, 3).reshape(FT0 * G_GU, 256),
        "qz_gu": pad_f(v["L0_ffn_qzeros_gu"]).reshape(G_GU, -1),
        "qw_dn": qd.transpose(1, 2, 0, 3),
        "sc_dn": v["L0_ffn_scales_down"].reshape(G_DN, KD, P).transpose(1, 0, 2).reshape(KD * G_DN, P),
        "qz_dn": v["L0_ffn_qzeros_down"],
        "gidx": np.concatenate([v["L0_ffn_g_idx_gu"][k_of], gd.reshape(FT0, P).T], axis=1),
        "ids": v["itok_B_0_7"],
        "aids": v["itok_B_3_7"],
        "w1T": v["L1_cond_weight"].transpose(0, 2, 1).reshape(NBATCH, KD, P, D).transpose(0, 2, 1, 3).reshape(NBATCH, P, KD * D),
        "lnw": v["L1_ffn_ln_w"].reshape(KD, P).T,
        "gu1": gu1.transpose(1, 4, 3, 0, 2).reshape(FT1, P, KD * 2 * P),
        "d1": v["L1_ffn_down_w"].reshape(KD, P, FT1, P).transpose(0, 3, 2, 1).reshape(KD, P, FT1 * P),
        "cst": cst,
        "shifts": np.stack([4 * (p // 64), 4 * (p % 8)], axis=1).astype(np.uint32),
    }
    nc = bacc.Bacc("TRN2", target_bir_lowering=False, num_devices=1)
    feed, aps = {}, {}
    for name, arr in arrays.items():
        arr = np.ascontiguousarray(arr)
        feed[f"in_{name}"] = arr
        aps[name] = nc.dram_tensor(f"in_{name}", arr.shape, mybir.dt.from_np(arr.dtype), kind="ExternalInput").ap()
    out = nc.dram_tensor("out_T", (KD, P, T), F32, kind="ExternalOutput").ap()
    build(nc, aps, out)
    r = run_bass_kernel_spmd(nc, [feed], core_ids=[0])
    got = r.results[0]["out_T"]
    return got.reshape(D, T).T.reshape(NBATCH, SEQ, D)
```

```python
from contextlib import ExitStack

import concourse.bass as bass
import numpy as np
from concourse import mybir

F32 = mybir.dt.float32
F32R = mybir.dt.float32r
BF16 = mybir.dt.bfloat16
I32 = mybir.dt.int32
U32 = mybir.dt.uint32
U8 = mybir.dt.uint8
ALU = mybir.AluOpType
ACT = mybir.ActivationFunctionType
AX = mybir.AxisListType

P = 128
NBATCH, SEQ, D = 8, 128, 512
T = NBATCH * SEQ
HALF = 512
NH = T // HALF
KD = D // P
E, R = 8, 16
LANG_BIAS, SCALING = 5.0, 2.0
GROUP = 128
F0 = 1376
FT0 = -(-F0 // P)
G_GU, G_DN = D // GROUP, F0 // GROUP
F1 = 1792
FT1 = F1 // P
CH0 = (6, 5)
CH1 = (7, 7)
EPS = 1e-5
YT = 11
C_ID, C_IOTA, C_OGU, C_ODN, C_END = 0, 128, 136, 136 + 44, 136 + 44 + 44


def need(eng, sem, value):
    if not isinstance(value, int) or value > 0:
        eng.wait_ge(sem, value)


def halves(ap):
    return ap.rearrange("p (h t) -> p h t", h=NH)


def build(nc, a, out):
    with ExitStack() as ctx:
        def sb(name, shape, dt):
            return ctx.enter_context(nc.sbuf_tensor(name, shape, dt))

        def sem(name):
            return ctx.enter_context(nc.semaphore(name))

        def over(name, shape, dt):
            with nc.sbuf_tensor(name, shape, dt) as t:
                return t

        adapter_a = over("adapter_a", [P, 2, KD * D], F32)
        act_hi = sb("act_hi", [P, KD, T], F32R)
        dn_work = over("dn_work", [P, 2816], F32)
        act_lo = sb("act_lo", [P, KD, T], F32R)
        adapter_b = over("adapter_b", [P, 5, KD * D], F32)
        h_hi = sb("h_hi", [P, YT + 4, T], F32R)
        adapter_c = over("adapter_c", [P, 1, KD * D], F32)
        h_lo = sb("h_lo", [P, YT + 4, T], F32R)
        ring_hi = sb("ring_hi", [P, 2, 1024], F32R)
        ring_lo = sb("ring_lo", [P, 2, 1024], F32R)
        raw = sb("raw", [P, 2, 1024], F32)
        sil = sb("sil", [P, 2, 1024], F32)
        res = sb("res", [P, KD, T], F32)
        cst = sb("cst", [P, C_END], F32)
        shifts = sb("shifts", [P, 2], U32)
        sh8 = shifts[:, 0:1].bitcast(U8)[:, 0:1]
        sh32 = shifts[:, 1:2]
        gidx = sb("gidx", [P, KD + FT0], I32)
        idx_gu = sb("idx_gu", [P, FT0, KD], I32)
        idx_dn = sb("idx_dn", [P, KD, FT0], I32)
        idx_cur = sb("idx_cur", [P, 2, 8], I32)
        ids = sb("ids", [P, NBATCH], I32)
        aid = sb("aid", [1, 3 * NBATCH], I32)
        aidf = sb("aidf", [1, 2 * NBATCH], F32)
        lnw = sb("lnw", [P, KD], F32)
        col = sb("col", [P, 8], F32)
        wr = sb("wr", [P, KD, E], F32)

        ident = cst[:, C_ID:C_ID + P]
        work = res[:, :, :].rearrange("p k t -> p (k t)")
        ZW = FT0 * 16
        at = KD * 2 * ZW
        zgp = work[:, 0:at].bitcast(U32)
        nib_gu = work[:, at:at + 256].bitcast(U8)
        z_gu = work[:, at + 256:at + 512].bitcast(U8)
        n_gu = work[:, at + 512:at + 1024].bitcast(BF16)
        qw = [work[:, at + 1024 + 256 * s:at + 1280 + 256 * s].bitcast(U32) for s in range(2)]
        zdp = dn_work[:, 0:704].bitcast(U32).rearrange("p (k w) -> p k w", k=FT0)
        z_dn = dn_work[:, 704:896].bitcast(U8)
        n_dn = dn_work[:, 896:1280].bitcast(BF16)
        qd = dn_work[:, 1280:2816].bitcast(U32).rearrange("p (s n) -> p s n", s=2)
        raw_w = raw[:, :, :].rearrange("p s n -> p (s n)")
        w0_hi, w0_lo = (t[:, 0:2, :].rearrange("p a (b n) -> p (a b) n", n=D) for t in (h_hi, h_lo))
        a_hi, a_lo = (t[:, 2, 0:512].rearrange("p (k n) -> p k n", n=P) for t in (h_hi, h_lo))
        b_hi, b_lo = (t[:, 2, 512:1024] for t in (h_hi, h_lo))
        hg_hi, hg_lo = (t[:, 3, :] for t in (h_hi, h_lo))
        ab_raw = sil[:, 0, :]
        hg_full = sil[:, 0, :]
        g_exp = raw[:, 0, :]
        g_T = raw[:, 1, :]
        gt = sil[:, 1, :]
        L_log, L_mx, L_eq, L_g1, L_g2 = (gt[:, 64 * i:64 * i + 64] for i in range(5))
        L_mi = gt[:, 320:384].bitcast(U32)
        L_mif, L_idf, L_w = gt[:, 384:448], gt[:, 448:456], gt[:, 456:512]
        idxf = gt[:, 512:640]

        ps = ctx.enter_context(nc.psum_tensor("ps", [P, 8, HALF], F32))

        s_x = [sem(f"s_x{k}") for k in range(KD)]
        s_w0 = [sem(f"s_w0{c}") for c in range(2)]
        s_wr, s_b, s_ab, s_cst, s_sh, s_gi, s_id, s_aid, s_ln = (
            sem(n) for n in ("s_wr", "s_b", "s_ab", "s_cst", "s_sh", "s_gi", "s_id", "s_aid", "s_ln"))
        s_xhi, s_xlo, s_whi0, s_wlo0 = (sem(n) for n in ("s_xhi", "s_xlo", "s_whi0", "s_wlo0"))
        s_log, s_hA, s_gate_c, s_exp, s_gex, s_gTp, s_gT, s_hg, s_hghi, s_hglo = (
            sem(n) for n in ("s_log", "s_hA", "s_gate_c", "s_exp", "s_gex", "s_gTp", "s_gT", "s_hg", "s_hghi", "s_hglo"))
        s_y, s_yhi, s_ylo = (sem(n) for n in ("s_y", "s_yhi", "s_ylo"))
        s_idx, s_idc, s_zg, s_zd, s_aok = (sem(n) for n in ("s_idx", "s_idc", "s_zg", "s_zd", "s_aok"))
        s_v = sem("s_v")
        s_raw = {p: [sem(f"s_raw_{p}{s}") for s in range(2)] for p in ("gu0", "d0", "gu1", "d1")}
        s_qw = {p: [sem(f"s_qw_{p}{s}") for s in range(2)] for p in ("gu0", "d0")}
        s_nib, s_zl, s_zh, s_n, s_wf = (sem(n) for n in ("s_nib", "s_zl", "s_zh", "s_n", "s_wf"))
        s_whi = sem("s_whi")
        s_wlo = sem("s_wlo")
        s_gate = sem("s_gate")
        s_ring = sem("s_ring")
        s_silu, s_hm, s_hhi, s_hlo = (sem(n) for n in ("s_silu", "s_hm", "s_hhi", "s_hlo"))
        s_res = sem("s_res")
        s_xr = sem("s_xr")
        s_rhi, s_rlo, s_sq, s_rc, s_rs, s_zs, s_zt, s_nx, s_nhi, s_nlo, s_vv = (
            sem(n) for n in ("s_rhi", "s_rlo", "s_sq", "s_rc", "s_rs", "s_zs", "s_zt", "s_nx", "s_nhi", "s_nlo", "s_vv"))
        s_a0, s_a1, s_a7 = sem("s_a0"), sem("s_a1"), sem("s_a7")
        s_a2 = sem("s_a2")
        s_abs = [sem("s_a35"), sem("s_a46")]
        s_ahi, s_alo, s_alp = sem("s_ahi"), sem("s_alo"), sem("s_alp")
        s_dlast = sem("s_dlast")
        s_last = sem("s_last")
        s_out = sem("s_out")

        Q = {"gu0": 0, "d0": FT0, "gu1": FT0 + 8, "d1": FT0 + 8 + FT1}
        N = {"gu0": 0, "d0": FT0, "c": FT0 + 8, "gu1": FT0 + 8 + NBATCH, "d1": FT0 + 8 + NBATCH + FT1}

        def loop(eng, start, end):
            return nc.Fori(start, end, engines=[eng.engine], hint_back_edge=True)

        def adapter_raw(b):
            if isinstance(b, int) and b < 2:
                return adapter_a[:, b, :]
            if isinstance(b, int) and b == NBATCH - 1:
                return adapter_c[:, 0, :]
            return adapter_b[:, bass.ds(b - 2, 1), :].rearrange("p o n -> p (o n)")

        def raw_free(eng, q):
            need(eng, s_whi, q - 1)
            need(eng, s_wlo, q - 1)

        block = ctx.enter_context(nc.Block())

        @block.sync
        def _(sp):
            sp.dma_start(ab_raw[:, 0:512], a["aT"]).then_inc(s_ab, 16)
            for k in range(KD):
                sp.dma_start(res[:, k, :], a["xT"][:, k, :]).then_inc(s_x[k], 16)
            sp.dma_start(wr[:, :, :], a["wrT"]).then_inc(s_wr, 16)
            for c in range(2):
                sp.dma_start(raw[:, c, :], a["w0T"][:, 1024 * c:1024 * c + 1024]).then_inc(s_w0[c], 16)
            sp.dma_start(ab_raw[:, 512:1024], a["bT"]).then_inc(s_b, 16)

            def load_gu1(i, s):
                raw_free(sp, i + Q["gu1"])
                sp.dma_start(raw[:, 1 - s, :], a["gu1"][bass.ds(i, 1), :, :].rearrange("o p n -> (o p) n")
                             ).then_inc(s_raw["gu1"][s], 16)

            def load_qw(i, s):
                for hp in range(2):
                    sp.dma_start(qw[s][64 * hp:64 * hp + 64, :], a["qw_gu"][bass.ds(i, 1), :, :].rearrange("o r c -> (o r) c")
                                 ).then_inc(s_qw["gu0"][s], 16)

            sp.wait_ge(s_xlo, KD)
            sp.wait_ge(s_xhi, KD)
            sp.wait_ge(s_log, 1)
            for i in range(2):
                load_qw(i, i)
            with loop(sp, 0, (FT0 - 3) // 2) as j:
                for s in range(2):
                    need(sp, s_nib, 2 * j + s + 1)
                    load_qw(2 * j + s + 2, s)
            need(sp, s_nib, FT0 - 2)
            load_qw(FT0 - 1, (FT0 - 1) % 2)

            def load_qd(m, c):
                k0, cnt = CH0[0] * c, CH0[c]
                sp.dma_start(qd[:, c, 0:cnt * P].rearrange("p (k n) -> p k n", n=P),
                             a["qw_dn"][:, bass.ds(m, 1), k0:k0 + cnt, :].rearrange("p o k n -> p (o k) n")
                             ).then_inc(s_qw["d0"][c], 16)

            sp.wait_ge(s_y, KD)
            for c in range(2):
                load_qd(0, c)
            need(sp, s_wf, FT0)
            sp.dma_start(res[:, :, :], a["xT"]).then_inc(s_xr, 16)

            sp.wait_ge(s_aok, 1)

            def load_adapter(b, done):
                row = sp.value_load(aid[0:1, bass.ds(b + 2 * NBATCH, 1)], min_val=0, max_val=NBATCH - 1)
                sp.dma_start(adapter_raw(b), a["w1T"][bass.ds(row, 1), :, :].rearrange("o p n -> (o p) n")
                             ).then_inc(done, 16)

            load_adapter(0, s_a0)
            load_adapter(1, s_a1)
            with loop(sp, 1, KD) as m:
                for c in range(2):
                    need(sp, s_n, FT0 + 2 * m + c - 1)
                    load_qd(m, c)
            for i in range(2):
                load_gu1(i, i)
            sp.wait_ge(s_ring, N["c"])
            load_adapter(2, s_a2)
            with loop(sp, 1, NBATCH // 2 - 1) as j:
                for s in range(2):
                    if True:
                        need(sp, s_ahi, 2 * j + s) 
                    load_adapter(2 * j + s + 1, s_abs[s])
            load_adapter(NBATCH - 1, s_a7)

            with loop(sp, 1, FT1 // 2) as j:
                for s in range(2):
                    load_gu1(2 * j + s, s)
            with loop(sp, 0, KD) as m:
                for c in range(2):
                    n = CH1[c] * P
                    raw_free(sp, 2 * m + c + Q["d1"])
                    sp.dma_start(raw[:, 1 - c, 0:n], a["d1"][bass.ds(m, 1), :, n * c:n * c + n].rearrange("o p n -> (o p) n")
                                 ).then_inc(s_raw["d1"][c], 16)
            with loop(sp, 0, KD - 1) as m:
                sp.wait_ge(s_res, m + KD + 1)
                sp.dma_start(out[bass.ds(m, 1), :, :].rearrange("o p t -> (o p) t"), res[:, bass.ds(m, 1), :].rearrange(
                    "p o t -> p (o t)")).then_inc(s_out, 16)
            for hf in range(NH):
                sp.wait_ge(s_last, hf + 1)
                t = slice(HALF * hf, HALF * hf + HALF)
                sp.dma_start(out[KD - 1, :, t], res[:, KD - 1, t]).then_inc(s_out, 16)
            sp.wait_ge(s_out, 16 * (KD + 1))

        @block.gpsimd
        def _(pool):
            pool.dma_start(cst[:, :], a["cst"]).then_inc(s_cst, 16)
            pool.dma_start(gidx[:, :], a["gidx"]).then_inc(s_gi, 16)
            pool.dma_start(ids[:, :], a["ids"].partition_broadcast(P)).then_inc(s_id, 16)
            pool.dma_start(aid[:, 0:NBATCH], a["aids"].partition_broadcast(1)).then_inc(s_aid, 16)
            pool.dma_start(lnw[:, :], a["lnw"]).then_inc(s_ln, 16)
            pool.dma_start(shifts[:, :], a["shifts"]).then_inc(s_sh, 16)

            def gather(dst, table, index, done):
                pool.indirect_dma_start(dst, None, table, bass.IndirectOffsetOnAxis(ap=index, axis=0)).then_inc(done, 16)

            pool.wait_ge(s_idx, 2)
            pool.wait_ge(s_xlo, KD)
            pool.wait_ge(s_xhi, KD)
            pool.wait_ge(s_log, 1)
            for k in range(KD):
                gather(zgp[:, 2 * ZW * k:2 * ZW * (k + 1)], a["qz_gu"], idx_gu[:, 0, k:k + 1], s_zg)

            def scales_gu(i, s):
                raw_free(pool, i)
                pool.tensor_copy(idx_cur[:, s, 0:KD], idx_gu[:, bass.ds(i, 1), :].rearrange("p o k -> p (o k)")).then_inc(s_idc, 1)
                pool.drain()
                for k in range(KD):
                    gather(raw[:, s, 256 * k:256 * k + 256], a["sc_gu"], idx_cur[:, s, k:k + 1], s_raw["gu0"][s])

            pool.wait_ge(s_hg, 1)
            for i in range(2):
                scales_gu(i, i)
            pool.wait_ge(s_y, KD)
            for i in range(FT0):
                gather(zdp[:, i, :], a["qz_dn"], idx_dn[:, 0, i:i + 1], s_zd)
            with loop(pool, 1, FT0 // 2) as j:
                for s in range(2):
                    scales_gu(2 * j + s, s)
            scales_gu(FT0 - 1, 0)

            with loop(pool, 0, KD) as m:
                for c in range(2):
                    k0, cnt = CH0[0] * c, CH0[c]
                    raw_free(pool, 2 * m + c + Q["d0"])
                    pool.tensor_copy(idx_cur[:, 1 - c, 0:cnt], idx_dn[:, bass.ds(m, 1), k0:k0 + cnt].rearrange("p o k -> p (o k)")
                                     ).then_inc(s_idc, 1)
                    pool.drain()
                    for k in range(cnt):
                        gather(raw[:, 1 - c, P * k:P * k + P], a["sc_dn"], idx_cur[:, 1 - c, k:k + 1], s_raw["d0"][c])

            for b in range(NBATCH):
                at_h = YT + 2 * (b % 2) + 1
                pool.wait_ge(s_ahi, b + 1)
                pool.tensor_tensor(h_lo[:, at_h, :], adapter_raw(b)[:, T:2 * T], h_hi[:, at_h, :].bitcast(F32),
                                   ALU.subtract).then_inc(s_alp, 1)
                pool.wait_ge(s_rhi, b + 1)
                r_hi, r_lo = (t[:, 1 - b % 2, 0:D].rearrange("p (k t) -> p k t", k=KD) for t in (ring_hi, ring_lo))
                pool.tensor_tensor(r_lo, res[:, :, SEQ * b:SEQ * b + SEQ], r_hi.bitcast(F32), ALU.subtract).then_inc(s_rlo, 1)

        @block.scalar
        def _(act):
            def hi(dst, src, done):
                act.activation(dst, src, ACT.Copy).then_inc(done, 1)

            act.wait_ge(s_ab, 16)
            hi(h_hi[:, 2, 0:512], ab_raw[:, 0:512], s_whi0)
            for k in range(KD):
                act.wait_ge(s_x[k], 16)
                hi(act_hi[:, k, :], res[:, k, :], s_xhi)
            for c in range(2):
                act.wait_ge(s_w0[c], 16)
                hi(h_hi[:, c, :], raw[:, c, :], s_whi0)
            act.wait_ge(s_b, 16)
            hi(h_hi[:, 2, 512:1024], ab_raw[:, 512:1024], s_whi0)
            act.wait_ge(s_gate_c, 1)
            act.activation(L_w[:, 8:16], L_w[:, 0:8], ACT.Exp).then_inc(s_exp, 1)
            act.wait_ge(s_gTp, 1)
            act.activation(halves(g_T), ps[:, 2:4, :], ACT.Copy).then_inc(s_gT, 1)
            act.wait_ge(s_hg, 1)
            hi(hg_hi, hg_full, s_hghi)

            def y_split(m, b):
                act.wait_ge(s_y, m + 1)
                hi(halves(h_hi[:, YT + m, :]), ps[:, b:b + 2, :], s_yhi)

            def w_hi(q, n, s, width, loaded, value):
                need(act, loaded, value)
                need(act, s_ring, n - 1)
                hi(ring_hi[:, s, 0:width], raw[:, s, 0:width], s_whi)

            def w_hi_gu(ph, i, s):
                if ph == "gu0":
                    w_hi(i, i, s, 1024, s_wf, i + 1)
                else:
                    w_hi(i + Q[ph], i + N[ph], 1 - s, 1024, s_raw[ph][s], (i - s) * 8 + 16)

            def w_hi_dn(ph, m, c):
                if ph == "d0":
                    w_hi(2 * m + c + Q[ph], 2 * m + c + N[ph], 1 - c, CH0[c] * P, s_wf, FT0 + 2 * m + c + 1)
                else:
                    w_hi(2 * m + c + Q[ph], 2 * m + c + N[ph], 1 - c, CH1[c] * P, s_raw[ph][c], 16 * m + 16)

            def silu(i, s, base):
                need(act, s_gate, i + base + 1)
                need(act, s_hlo, i + base - 1)
                act.activation(halves(sil[:, s, :]), ps[:, 4 * s:4 * s + 2, :], ACT.Silu).then_inc(s_silu, 1)

            def h_split(i, s, base):
                need(act, s_hm, i + base + 1)
                hi(h_hi[:, bass.ds(i, 1), :].rearrange("p o t -> p (o t)"), sil[:, s, :], s_hhi)

            def gu_step(ph, i, s, base, then):
                then()
                silu(i, s, base)
                h_split(i, s, base)

            y_split(0, 0)
            y_split(1, 4)
            w_hi_gu("gu0", 0, 0)
            y_split(2, 6)
            y_split(3, 2)
            for i in range(2):
                gu_step("gu0", i, i, 0, lambda: w_hi_gu("gu0", i + 1, 1 - i))
            with loop(act, 1, FT0 // 2) as j:
                for s in range(2):
                    i = 2 * j + s
                    gu_step("gu0", i, s, 0, lambda: w_hi_gu("gu0", i + 1, 1 - s))
            gu_step("gu0", FT0 - 1, 0, 0, lambda: w_hi_dn("d0", 0, 0))

            w_hi_dn("d0", 0, 1)
            with loop(act, 1, KD) as m:
                for c in range(2):
                    w_hi_dn("d0", m, c)

            def batch_a(b, s, done, value=16):
                act.wait_ge(done, value)
                need(act, s_ring, max(b + N["c"] - 1, 0) if isinstance(b, int) and b >= 2 else
                     (FT0 if isinstance(b, int) else b + N["c"] - 1))
                hi(h_hi[:, YT + 2 * s:YT + 2 * s + 2, :].rearrange("p a n -> p (a n)"), adapter_raw(b), s_ahi)

            def batch_z(b, s):
                need(act, s_ring, b + N["c"] + 1)
                need(act, s_zt, b - 1)
                act.activation(sil[:, s, 0:D], ps[:, 4 + s, :], ACT.Square, accum_out=col[:, s:s + 1]).then_inc(s_sq, 1)

            def batch_n(b, s):
                need(act, s_nx, b + 1)
                hi(act_hi[:, :, bass.ds(b * SEQ, SEQ)], sil[:, s, D:2 * D].rearrange("p (k t) -> p k t", k=KD), s_nhi)

            def batch_r(b, s):
                need(act, s_rc, b + 1)
                act.activation(col[:, 4 + s:5 + s], col[:, 2 + s:3 + s], ACT.Sqrt).then_inc(s_rs, 1)

            batch_a(0, 0, s_a0)
            batch_a(1, 1, s_a1)
            batch_z(0, 0)
            batch_r(0, 0)
            batch_a(2, 0, s_a2)
            batch_z(1, 1)
            batch_n(0, 0)
            batch_r(1, 1)
            with loop(act, 1, NBATCH // 2 - 1) as j:
                for s in range(2):
                    b = 2 * j + s
                    batch_a(b + 1, 1 - s, s_abs[s], 16 * j)
                    batch_z(b, s)
                    batch_n(b - 1, 1 - s)
                    batch_r(b, s)
            batch_a(7, 1, s_a7)
            for b in range(NBATCH - 2, NBATCH):
                batch_z(b, b % 2)
                batch_n(b - 1, 1 - b % 2)
                batch_r(b, b % 2)
            w_hi_gu("gu1", 0, 0)
            batch_n(NBATCH - 1, 1)

            for i in range(2):
                gu_step("gu1", i, i, FT0, lambda: w_hi_gu("gu1", i + 1, 1 - i))
            with loop(act, 1, FT1 // 2 - 1) as j:
                for s in range(2):
                    i = 2 * j + s
                    gu_step("gu1", i, s, FT0, lambda: w_hi_gu("gu1", i + 1, 1 - s))
            gu_step("gu1", FT1 - 2, 0, FT0, lambda: w_hi_gu("gu1", FT1 - 1, 1))
            gu_step("gu1", FT1 - 1, 1, FT0, lambda: w_hi_dn("d1", 0, 0))
            w_hi_dn("d1", 0, 1)
            with loop(act, 1, KD) as m:
                for c in range(2):
                    w_hi_dn("d1", m, c)

        @block.vector
        def _(dve):
            done = [0]

            def own(ins):
                done[0] += 1
                ins.then_inc(s_v, 1)
                dve.wait_ge(s_v, done[0])

            def lo(dst, src, hi_part, done_sem):
                dve.tensor_tensor(dst, src, hi_part.bitcast(F32), ALU.subtract).then_inc(done_sem, 1)

            dve.wait_ge(s_whi0, 1)
            lo(h_lo[:, 2, 0:512], ab_raw[:, 0:512], h_hi[:, 2, 0:512], s_wlo0)
            for k in range(KD):
                dve.wait_ge(s_xhi, k + 1)
                lo(act_lo[:, k, :], res[:, k, :], act_hi[:, k, :], s_xlo)
            for c in range(2):
                dve.wait_ge(s_whi0, 2 + c)
                lo(h_lo[:, c, :], raw[:, c, :], h_hi[:, c, :], s_wlo0)
            dve.wait_ge(s_whi0, 4)
            lo(h_lo[:, 2, 512:1024], ab_raw[:, 512:1024], h_hi[:, 2, 512:1024], s_wlo0)

            dve.wait_ge(s_gi, 16)
            dve.wait_ge(s_cst, 16)
            g_f, g_n = idxf[:, 0:15], idxf[:, 16:31]
            own(dve.tensor_copy(g_f, gidx[:, :]))
            for lo_c, hi_c, n in ((0, KD, G_GU), (KD, KD + FT0, G_DN)):
                own(dve.tensor_scalar(g_n[:, lo_c:hi_c], g_f[:, lo_c:hi_c], 0.0, float(n), ALU.is_lt, ALU.mult))
                own(dve.tensor_tensor(g_n[:, lo_c:hi_c], g_f[:, lo_c:hi_c], g_n[:, lo_c:hi_c], ALU.add))
                own(dve.tensor_scalar(g_n[:, lo_c:hi_c], g_n[:, lo_c:hi_c], 0.0, float(n - 1), ALU.max, ALU.min))
            dve.tensor_tensor(idx_gu[:, :, :], g_n[:, 0:KD].unsqueeze(1).to_broadcast([P, FT0, KD]),
                              cst[:, C_OGU:C_ODN].rearrange("p (i k) -> p i k", k=KD), ALU.add).then_inc(s_idx, 1)
            dve.tensor_tensor(idx_dn[:, :, :], g_n[:, KD:KD + FT0].unsqueeze(1).to_broadcast([P, KD, FT0]),
                              cst[:, C_ODN:C_END].rearrange("p (m i) -> p m i", i=FT0), ALU.add).then_inc(s_idx, 1)
            dve.wait_ge(s_aid, 16)
            a_f, a_n = aidf[:, 0:NBATCH], aidf[:, NBATCH:2 * NBATCH]
            own(dve.tensor_copy(a_f, aid[:, 0:NBATCH]))
            own(dve.tensor_scalar(a_n, a_f, 0.0, float(NBATCH), ALU.is_lt, ALU.mult))
            own(dve.tensor_tensor(a_n, a_f, a_n, ALU.add))
            dve.tensor_scalar(aid[:, 2 * NBATCH:3 * NBATCH], a_n, 0.0, float(NBATCH - 1), ALU.max, ALU.min).then_inc(s_aok, 1)


            def g3(ap):
                return ap.rearrange("p (b e) -> p b e", e=E)

            iota = cst[:, C_IOTA:C_IOTA + E].unsqueeze(1).to_broadcast([P, NBATCH, E])

            def per_batch(ap):
                return ap.unsqueeze(2).to_broadcast([P, NBATCH, E])

            dve.wait_ge(s_id, 16)
            own(dve.tensor_copy(L_idf, ids[:, :]))
            own(dve.tensor_tensor(g3(L_eq), per_batch(L_idf), iota, ALU.is_equal))
            dve.wait_ge(s_log, 1)
            own(dve.scalar_tensor_tensor(out=L_log, in0=L_eq, scalar=LANG_BIAS, in1=ps[:, 2, 0:64],
                                         op0=ALU.mult, op1=ALU.add))
            for b in range(NBATCH):
                ins = dve.max(L_mx[:, 8 * b:8 * b + 8], L_log[:, 8 * b:8 * b + 8])
            own(ins)
            for b in range(NBATCH):
                ins = dve.max_index(L_mi[:, 8 * b:8 * b + 8], L_mx[:, 8 * b:8 * b + 8], L_log[:, 8 * b:8 * b + 8])
            own(ins)
            dve.tensor_tensor(L_w[:, 0:8], g3(L_mx)[:, :, 1], g3(L_mx)[:, :, 0], ALU.subtract).then_inc(s_gate_c, 1)
            own(dve.tensor_copy(L_mif, L_mi))
            own(dve.tensor_tensor(g3(L_g1), per_batch(g3(L_mif)[:, :, 0]), iota, ALU.is_equal))
            own(dve.tensor_tensor(g3(L_g2), per_batch(g3(L_mif)[:, :, 1]), iota, ALU.is_equal))
            dve.wait_ge(s_exp, 1)
            own(dve.tensor_scalar(L_w[:, 16:24], L_w[:, 8:16], 1.0, None, ALU.add))
            own(dve.reciprocal(L_w[:, 24:32], L_w[:, 16:24]))
            own(dve.tensor_scalar(L_w[:, 32:40], L_w[:, 24:32], SCALING, None, ALU.mult))
            own(dve.tensor_tensor(L_w[:, 40:48], L_w[:, 32:40], L_w[:, 8:16], ALU.mult))
            own(dve.tensor_tensor(g3(L_g1), g3(L_g1), per_batch(L_w[:, 32:40]), ALU.mult))
            own(dve.tensor_tensor(g3(L_g2), g3(L_g2), per_batch(L_w[:, 40:48]), ALU.mult))
            own(dve.tensor_tensor(L_g1, L_g1, L_g2, ALU.add))
            dve.wait_ge(s_wlo0, 4)
            dve.tensor_copy(g_exp.rearrange("p (g r) -> p g r", r=R),
                            L_g1.unsqueeze(2).to_broadcast([P, NBATCH * E, R])).then_inc(s_gex, 1)
            dve.wait_ge(s_gT, 1)
            dve.wait_ge(s_hA, 1)
            dve.tensor_tensor(halves(hg_full), ps[:, 6:8, :], halves(g_T), ALU.mult).then_inc(s_hg, 1)
            dve.wait_ge(s_hghi, 1)
            lo(hg_lo, hg_full, hg_hi, s_hglo)

            def y_split(m, b):
                dve.wait_ge(s_yhi, m + 1)
                lo(halves(h_lo[:, YT + m, :]), ps[:, b:b + 2, :], halves(h_hi[:, YT + m, :]), s_ylo)

            def w_lo(q, s, width):
                need(dve, s_whi, q + 1)
                lo(ring_lo[:, s, 0:width], raw[:, s, 0:width], ring_hi[:, s, 0:width], s_wlo)

            dve.wait_ge(s_sh, 16)
            dve.wait_ge(s_zg, 16 * KD)
            zg8 = zgp.bitcast(U8).rearrange("p (g w) -> p g w", g=2 * KD)
            z3 = z_gu.rearrange("p (g w e) -> p g w e", g=2 * KD, e=2)

            def dequant_gu(i, s):
                need(dve, s_qw["gu0"][s], (i - s) * 16 + 32)
                need(dve, s_n, i)
                words = qw[s].bitcast(U8).rearrange("p (c j) -> p j c", j=4)
                dve.tensor_scalar(nib_gu.rearrange("p (j c) -> p j c", j=4), words, sh8, 15,
                                  ALU.logical_shift_right, ALU.bitwise_and).then_inc(s_nib, 1)
                zw = zg8[:, :, bass.ds(i * 64, 64)]
                dve.tensor_scalar(z3[:, :, :, 0], zw, 15, None, ALU.bitwise_and).then_inc(s_zl, 1)
                dve.tensor_scalar(z3[:, :, :, 1], zw, 4, None, ALU.logical_shift_right).then_inc(s_zh, 1)
                need(dve, s_nib, i + 1)
                need(dve, s_zl, i + 1)
                need(dve, s_zh, i + 1)
                need(dve, s_wf, i)
                dve.scalar_tensor_tensor(out=n_gu, in0=nib_gu, scalar=1.0, in1=z_gu, op0=ALU.subtract,
                                         op1=ALU.subtract).then_inc(s_n, 1)
                need(dve, s_n, i + 1)
                need(dve, s_raw["gu0"][s], (i - s) * 32 + 64)
                dve.tensor_tensor(raw[:, s, :], raw[:, s, :], n_gu, ALU.mult).then_inc(s_wf, 1)

            def dequant_dn(m, c):
                k0, cnt = CH0[0] * c, CH0[c]
                e = 2 * m + c + FT0
                need(dve, s_qw["d0"][c], 16 * m + 16)
                q = qd[:, c, 0:cnt * P]
                dve.tensor_scalar(q, q, sh32, 15, ALU.logical_shift_right, ALU.bitwise_and).then_inc(s_nib, 1)
                zw = zdp[:, k0:k0 + cnt, :].bitcast(U8)[:, :, bass.ds(m * 64, 64)]
                z4 = z_dn[:, 0:cnt * P].rearrange("p (k w e) -> p k w e", k=cnt, e=2)
                need(dve, s_n, e)
                dve.tensor_scalar(z4[:, :, :, 0], zw, 15, None, ALU.bitwise_and).then_inc(s_zl, 1)
                dve.tensor_scalar(z4[:, :, :, 1], zw, 4, None, ALU.logical_shift_right).then_inc(s_zh, 1)
                need(dve, s_nib, e + 1)
                need(dve, s_zl, e + 1)
                need(dve, s_zh, e + 1)
                need(dve, s_wf, e)
                dve.scalar_tensor_tensor(out=n_dn[:, 0:cnt * P], in0=q, scalar=1.0, in1=z_dn[:, 0:cnt * P],
                                         op0=ALU.subtract, op1=ALU.subtract).then_inc(s_n, 1)
                need(dve, s_n, e + 1)
                need(dve, s_raw["d0"][c], (m + 1) * (16 * cnt))
                dve.tensor_tensor(raw[:, 1 - c, 0:cnt * P], raw[:, 1 - c, 0:cnt * P], n_dn[:, 0:cnt * P],
                                  ALU.mult).then_inc(s_wf, 1)

            def h_step(i, s, base, nbase):
                need(dve, s_silu, i + base + 1)
                need(dve, s_ring, i + nbase + 1)
                dve.tensor_tensor(halves(sil[:, s, :]), halves(sil[:, s, :]), ps[:, 4 * s + 2:4 * s + 4, :],
                                  ALU.mult).then_inc(s_hm, 1)
                need(dve, s_hhi, i + base + 1)
                t = bass.ds(i, 1)
                lo(h_lo[:, t, :].rearrange("p o t -> p (o t)"), sil[:, s, :],
                   h_hi[:, t, :].rearrange("p o t -> p (o t)"), s_hlo)

            y_split(0, 0)
            y_split(1, 4)
            dequant_gu(0, 0)
            w_lo(0, 0, 1024)
            y_split(2, 6)
            y_split(3, 2)
            for i in range(2):
                dequant_gu(i + 1, 1 - i)
                w_lo(i + 1, 1 - i, 1024)
                h_step(i, i, 0, N["gu0"])
            with loop(dve, 1, FT0 // 2) as j:
                for s in range(2):
                    i = 2 * j + s
                    dequant_gu(i + 1, 1 - s)
                    w_lo(i + 1, 1 - s, 1024)
                    h_step(i, s, 0, N["gu0"])
            dve.wait_ge(s_zd, 16 * FT0)
            dequant_dn(0, 0)
            w_lo(Q["d0"], 1, CH0[0] * P)
            h_step(FT0 - 1, 0, 0, N["gu0"])

            def adapter_lo(b, s):
                need(dve, s_ahi, b + 1)
                lo(h_lo[:, YT + 2 * s, :], adapter_raw(b)[:, 0:T], h_hi[:, YT + 2 * s, :], s_alo)

            def down_chunk0(m, c):
                dequant_dn(m, c)
                w_lo(2 * m + c + Q["d0"], 1 - c, CH0[c] * P)

            def add_res(m, bank, n_last):
                need(dve, s_ring, n_last + 1)
                t = res[:, bass.ds(m, 1), :].rearrange("p o (h t) -> p (o h) t", h=NH)
                dve.tensor_tensor(t, ps[:, bank, :], t, ALU.add).then_inc(s_res, 1)

            down_chunk0(0, 1)
            dve.wait_ge(s_xr, 16)
            for m in range(KD):
                if m < KD - 1:
                    for c in range(2):
                        down_chunk0(m + 1, c)
                else:
                    for b in range(2):
                        adapter_lo(b, b)
                add_res(m, slice((4 + 2 * m) % 8, (4 + 2 * m) % 8 + 2), N["d0"] + 2 * m + 1)

            def split_r(b, s):
                need(dve, s_ring, b + N["c"] - 1)
                dve.tensor_copy(ring_hi[:, 1 - s, 0:D].rearrange("p (k t) -> p k t", k=KD),
                                res[:, :, bass.ds(b * SEQ, SEQ)]).then_inc(s_rhi, 1)

            def var(b, s):
                need(dve, s_sq, b + 1)
                dve.tensor_scalar(col[:, 6 + s:7 + s], col[:, s:s + 1], 1.0 / D, EPS, ALU.mult, ALU.add).then_inc(s_vv, 1)
                need(dve, s_vv, b + 1)
                dve.reciprocal(col[:, 2 + s:3 + s], col[:, 6 + s:7 + s]).then_inc(s_rc, 1)

            def norm(b, s):
                need(dve, s_rs, b + 1)
                dve.tensor_scalar(sil[:, s, 0:D], ps[:, 4 + s, :], col[:, 4 + s:5 + s], None, ALU.mult).then_inc(s_zs, 1)

            def weigh(b, s):
                need(dve, s_zt, b + 1)
                need(dve, s_nlo, b - 1)
                nx = sil[:, s, D:2 * D].rearrange("p (k t) -> p k t", k=KD)
                dve.tensor_tensor(nx, ps[:, 6 + s, :].rearrange("p (k t) -> p k t", k=KD),
                                  lnw[:, :].unsqueeze(2).to_broadcast([P, KD, SEQ]), ALU.mult).then_inc(s_nx, 1)
                need(dve, s_nhi, b + 1)
                t = bass.ds(b * SEQ, SEQ)
                lo(act_lo[:, :, t], nx, act_hi[:, :, t], s_nlo)

            dve.wait_ge(s_ln, 16)
            dve.wait_ge(s_res, KD)
            split_r(0, 0)
            split_r(1, 1)
            var(0, 0)
            norm(0, 0)
            adapter_lo(2, 0)
            split_r(2, 0)
            var(1, 1)
            weigh(0, 0)
            norm(1, 1)
            with loop(dve, 1, NBATCH // 2 - 1) as j:
                for s in range(2):
                    b = 2 * j + s
                    adapter_lo(b + 1, 1 - s)
                    split_r(b + 1, 1 - s)
                    var(b, s)
                    weigh(b - 1, 1 - s)
                    norm(b, s)
            adapter_lo(7, 1)
            split_r(7, 1)
            for b in range(NBATCH - 2, NBATCH):
                var(b, b % 2)
                weigh(b - 1, 1 - b % 2)
                norm(b, b % 2)
            w_lo(Q["gu1"], 1, 1024)
            weigh(NBATCH - 1, 1)

            def gu1_step(i, s):
                w_lo(i + 1 + Q["gu1"], s, 1024)
                h_step(i, s, FT0, N["gu1"])

            for i in range(2):
                gu1_step(i, i)
            with loop(dve, 1, FT1 // 2 - 1) as j:
                for s in range(2):
                    gu1_step(2 * j + s, s)
            gu1_step(FT1 - 2, 0)
            w_lo(Q["d1"], 1, CH1[0] * P)
            h_step(FT1 - 1, 1, FT0, N["gu1"])
            w_lo(Q["d1"] + 1, 0, CH1[1] * P)
            for m in range(KD):
                if m < KD - 1:
                    for c in range(2):
                        w_lo(2 * (m + 1) + c + Q["d1"], 1 - c, CH1[c] * P)
                    add_res(m, slice(2 * m, 2 * m + 2), N["d1"] + 2 * m + 1)
            for hf in range(NH):
                dve.wait_ge(s_dlast, hf + 1)
                t = slice(HALF * hf, HALF * hf + HALF)
                dve.tensor_tensor(res[:, KD - 1, t], ps[:, 2 * (KD - 1) + hf, :], res[:, KD - 1, t], ALU.add).then_inc(s_last, 1)

        @block.tensor
        def _(pe):
            def mm3(bank, w_hi, w_lo, v_hi, v_lo, first, last, hfs=range(NH)):
                for hf in hfs:
                    t = slice(HALF * hf, HALF * hf + HALF)
                    pe.matmul(ps[:, bank + hf, :], w_hi, v_hi[:, t], start=first, stop=False)
                    pe.matmul(ps[:, bank + hf, :], w_hi, v_lo[:, t], start=False, stop=False)
                for hf in hfs:
                    t = slice(HALF * hf, HALF * hf + HALF)
                    ins = pe.matmul(ps[:, bank + hf, :], w_lo, v_hi[:, t], start=False, stop=last)
                return ins

            for k in range(KD):
                pe.wait_ge(s_xhi, k + 1)
                pe.wait_ge(s_xlo, k + 1)
                if k == 0:
                    pe.wait_ge(s_wlo0, 1)
                ins = mm3(6, a_hi[:, k, :], a_lo[:, k, :], act_hi[:, k, :], act_lo[:, k, :], k == 0, k == KD - 1)
            ins.then_inc(s_hA, 1)
            pe.wait_ge(s_wr, 16)
            for b in range(NBATCH):
                for k in range(KD):
                    ins = pe.matmul(ps[:, 2, E * b:E * b + E], res[:, k, SEQ * b:SEQ * b + SEQ], wr[:, k, :],
                                    start=(k == 0), stop=(k == KD - 1))
            ins.then_inc(s_log, 1)

            def base(m, bank):
                for k in range(KD):
                    c = slice(P * m, P * m + P)
                    mm3(bank, w0_hi[:, k, c], w0_lo[:, k, c], act_hi[:, k, :], act_lo[:, k, :], k == 0, False)

            def lora(m, bank):
                c = slice(P * m, P * m + P)
                mm3(bank, b_hi[:, c], b_lo[:, c], hg_hi, hg_lo, False, True).then_inc(s_y, 1)

            pe.wait_ge(s_wlo0, 3)
            base(0, 0)
            pe.wait_ge(s_gex, 1)
            pe.wait_ge(s_cst, 16)
            for b in range(NBATCH):
                ins = pe.transpose(ps[:, 2 + b // 4, P * (b % 4):P * (b % 4) + P], g_exp[:, P * b:P * b + P], ident)
            ins.then_inc(s_gTp, 1)
            base(1, 4)
            pe.wait_ge(s_hglo, 1)
            lora(0, 0)
            lora(1, 4)
            base(2, 6)
            lora(2, 6)
            base(3, 2)
            lora(3, 2)

            def weights_ready(q):
                need(pe, s_whi, q + 1)
                need(pe, s_wlo, q + 1)

            def gate_up(q, s, i, slot, act_at, k_done=None):
                weights_ready(q)
                need(pe, s_hm, i - 1)
                for g in range(2):
                    for k in range(KD):
                        c = slice(256 * k + P * g, 256 * k + P * g + P)
                        if k_done is not None and g == 0:
                            pe.wait_ge(k_done, k + 1)
                        ins = mm3(4 * s + 2 * g, ring_hi[:, slot, c], ring_lo[:, slot, c],
                                  act_at[0][:, k, :], act_at[1][:, k, :], k == 0, k == KD - 1)
                    ins.then_inc(s_ring if g else s_gate, 1)

            y_at = (h_hi[:, YT:YT + KD, :], h_lo[:, YT:YT + KD, :])
            gate_up(0, 0, 0, 0, y_at, s_ylo)
            gate_up(1, 1, 1, 1, y_at)
            with loop(pe, 1, FT0 // 2) as j:
                for s in range(2):
                    gate_up(2 * j + s, s, 2 * j + s, s, y_at)
            gate_up(FT0 - 1, 0, FT0 - 1, 0, y_at)

            def down(m, q0, chunks, bank, h_done):
                for c in range(2):
                    weights_ready(q0 + 2 * m + c)
                    for k in range(chunks[c]):
                        i = chunks[0] * c + k
                        if m == 0:
                            pe.wait_ge(s_hhi, h_done + i + 1)
                            pe.wait_ge(s_hlo, h_done + i + 1)
                        w = slice(P * k, P * k + P)
                        ins = mm3(bank, ring_hi[:, 1 - c, w], ring_lo[:, 1 - c, w], h_hi[:, i, :], h_lo[:, i, :],
                                  i == 0, i == sum(chunks) - 1)
                    ins.then_inc(s_ring, 1)

            pe.wait_ge(s_hm, FT0 - 1)
            for m in range(KD):
                down(m, Q["d0"], CH0, (4 + 2 * m) % 8, 0)

            def z_product(b, s):
                need(pe, s_rhi, b + 1)
                need(pe, s_rlo, b + 1)
                need(pe, s_ahi, b + 1)
                need(pe, s_alo, b + 1)
                need(pe, s_alp, b + 1)
                need(pe, s_zs, b - 1)
                w_hi, w_lo = (t[:, YT + 2 * s:YT + 2 * s + 2, :].rearrange("p a (c n) -> p (a c) n", n=D)
                              for t in (h_hi, h_lo))
                for k in range(KD):
                    c = slice(SEQ * k, SEQ * k + SEQ)
                    pe.matmul(ps[:, 4 + s, :], ring_hi[:, 1 - s, c], w_hi[:, k, :], start=(k == 0), stop=False)
                    pe.matmul(ps[:, 4 + s, :], ring_hi[:, 1 - s, c], w_lo[:, k, :], start=False, stop=False)
                    ins = pe.matmul(ps[:, 4 + s, :], ring_lo[:, 1 - s, c], w_hi[:, k, :], start=False, stop=(k == KD - 1))
                ins.then_inc(s_ring, 1)

            def turn(b, s):
                need(pe, s_zs, b + 1)
                need(pe, s_nx, b - 1)
                for k in range(KD):
                    ins = pe.transpose(ps[:, 6 + s, P * k:P * k + P], sil[:, s, P * k:P * k + P], ident)
                ins.then_inc(s_zt, 1)

            z_product(0, 0)
            z_product(1, 1)
            turn(0, 0)
            with loop(pe, 1, NBATCH // 2) as j:
                for s in range(2):
                    z_product(2 * j + s, s)
                    turn(2 * j + s - 1, 1 - s)
            turn(NBATCH - 1, 1)

            z_at = (act_hi, act_lo)
            weights_ready(Q["gu1"])
            for hf in range(NH):
                pe.wait_ge(s_nhi, (hf + 1) * NBATCH // NH)
                pe.wait_ge(s_nlo, (hf + 1) * NBATCH // NH)
                for g in range(2):
                    for k in range(KD):
                        c = slice(256 * k + P * g, 256 * k + P * g + P)
                        ins = mm3(2 * g, ring_hi[:, 1, c], ring_lo[:, 1, c], act_hi[:, k, :], act_lo[:, k, :],
                                  k == 0, k == KD - 1, [hf])
                    if hf == NH - 1:
                        ins.then_inc(s_ring if g else s_gate, 1)
            gate_up(1 + Q["gu1"], 1, 1 + FT0, 0, z_at)
            with loop(pe, 1, FT1 // 2) as j:
                for s in range(2):
                    gate_up(2 * j + s + Q["gu1"], s, 2 * j + s + FT0, 1 - s, z_at)
            pe.wait_ge(s_hm, FT0 + FT1 - 1)
            for m in range(KD - 1):
                down(m, Q["d1"], CH1, 2 * m, FT0)
            m = KD - 1
            for c in range(2):
                weights_ready(Q["d1"] + 2 * m + c)
            for hf in range(NH):
                for i in range(FT1):
                    c, k = divmod(i, CH1[0])
                    w = slice(P * k, P * k + P)
                    ins = mm3(2 * m, ring_hi[:, 1 - c, w], ring_lo[:, 1 - c, w], h_hi[:, i, :], h_lo[:, i, :],
                              i == 0, i == FT1 - 1, [hf])
                ins.then_inc(s_dlast, 1)


def kernel(**inputs):
    import concourse.bacc as bacc
    from concourse.bass_utils import run_bass_kernel_spmd

    v = {k: np.asarray(x) for k, x in inputs.items()}
    p = np.arange(P)
    k_of = 8 * (p[:, None] % 64) + 2 * np.arange(KD)[None, :] + p[:, None] // 64

    def rows(w):
        return np.ascontiguousarray(w.reshape(-1, P, w.shape[1]).transpose(1, 0, 2).reshape(P, -1))

    def pad_f(w):
        w = w.reshape(*w.shape[:-1], 2, -1)
        width = FT0 * P * w.shape[-1] // F0 if w.shape[-1] == F0 else FT0 * 16
        return np.concatenate([w, np.zeros((*w.shape[:-1], width - w.shape[-1]), w.dtype)], axis=-1)

    order = k_of.T.reshape(-1)
    qg = pad_f(v["L0_ffn_qweight_gu"]).reshape(64, 2, FT0, P)
    sg = pad_f(v["L0_ffn_scales_gu"]).reshape(G_GU, 2, FT0, P)
    qd = np.repeat(v["L0_ffn_qweight_down"], 8, axis=0)
    qd = np.concatenate([qd, np.zeros((FT0 * P - F0, D), qd.dtype)]).reshape(FT0, P, KD, P)
    gd = np.concatenate([v["L0_ffn_g_idx_down"], np.zeros(FT0 * P - F0, v["L0_ffn_g_idx_down"].dtype)])
    gu1 = np.stack([v["L1_ffn_gate_w"].reshape(FT1, P, KD, P), v["L1_ffn_up_w"].reshape(FT1, P, KD, P)])
    cst = np.zeros((P, C_END), np.float32)
    cst[:, C_ID:C_ID + P] = np.eye(P)
    cst[:, C_IOTA:C_IOTA + E] = np.arange(E)
    cst[:, C_OGU:C_ODN] = np.repeat(G_GU * np.arange(FT0), KD)
    cst[:, C_ODN:C_END] = np.repeat(G_DN * np.arange(KD), FT0)
    arrays = {
        "xT": v["x"].reshape(T, KD, P).transpose(2, 1, 0),
        "wrT": rows(v["L0_cond_Wr"].T).reshape(P, KD, E),
        "aT": rows(v["L0_cond_A"].reshape(E * R, D).T),
        "w0T": rows(v["L0_cond_W"].T[:, order]),
        "bT": v["L0_cond_B"].transpose(0, 2, 1).reshape(E * R, D)[:, order],
        "qw_gu": qg.transpose(2, 0, 1, 3).reshape(FT0, 64, 256),
        "sc_gu": sg.transpose(2, 0, 1, 3).reshape(FT0 * G_GU, 256),
        "qz_gu": pad_f(v["L0_ffn_qzeros_gu"]).reshape(G_GU, -1),
        "qw_dn": qd.transpose(1, 2, 0, 3),
        "sc_dn": v["L0_ffn_scales_down"].reshape(G_DN, KD, P).transpose(1, 0, 2).reshape(KD * G_DN, P),
        "qz_dn": v["L0_ffn_qzeros_down"],
        "gidx": np.concatenate([v["L0_ffn_g_idx_gu"][k_of], gd.reshape(FT0, P).T], axis=1),
        "ids": v["itok_B_0_7"],
        "aids": v["itok_B_3_7"],
        "w1T": v["L1_cond_weight"].transpose(0, 2, 1).reshape(NBATCH, KD, P, D).transpose(0, 2, 1, 3).reshape(NBATCH, P, KD * D),
        "lnw": v["L1_ffn_ln_w"].reshape(KD, P).T,
        "gu1": gu1.transpose(1, 4, 3, 0, 2).reshape(FT1, P, KD * 2 * P),
        "d1": v["L1_ffn_down_w"].reshape(KD, P, FT1, P).transpose(0, 3, 2, 1).reshape(KD, P, FT1 * P),
        "cst": cst,
        "shifts": np.stack([4 * (p // 64), 4 * (p % 8)], axis=1).astype(np.uint32),
    }
    nc = bacc.Bacc("TRN2", target_bir_lowering=False, num_devices=1)
    feed, aps = {}, {}
    for name, arr in arrays.items():
        arr = np.ascontiguousarray(arr)
        feed[f"in_{name}"] = arr
        aps[name] = nc.dram_tensor(f"in_{name}", arr.shape, mybir.dt.from_np(arr.dtype), kind="ExternalInput").ap()
    out = nc.dram_tensor("out_T", (KD, P, T), F32, kind="ExternalOutput").ap()
    build(nc, aps, out)
    r = run_bass_kernel_spmd(nc, [feed], core_ids=[0])
    got = r.results[0]["out_T"]
    return got.reshape(D, T).T.reshape(NBATCH, SEQ, D)
```

```python
from contextlib import ExitStack

import concourse.bass as bass
import numpy as np
from concourse import mybir

F32 = mybir.dt.float32
F32R = mybir.dt.float32r
BF16 = mybir.dt.bfloat16
I32 = mybir.dt.int32
U32 = mybir.dt.uint32
U8 = mybir.dt.uint8
ALU = mybir.AluOpType
ACT = mybir.ActivationFunctionType

P = 128
NBATCH, SEQ, D = 8, 128, 512
T = NBATCH * SEQ
HALF = 512
NH = T // HALF
KD = D // P
E, R = 8, 16
LANG_BIAS, SCALING = 5.0, 2.0
GROUP = 128
F0 = 1376
FT0 = -(-F0 // P)
G_GU, G_DN = D // GROUP, F0 // GROUP
F1 = 1792
FT1 = F1 // P
CH0 = (6, 5)
CH1 = (7, 7)
EPS = 1e-5
YT = 11
C_ID, C_IOTA, C_OGU, C_END = 0, P, P + E, P + E + FT0 * KD


def need(eng, sem, value):
    if not isinstance(value, int) or value > 0:
        eng.wait_ge(sem, value)


def halves(ap):
    return ap.rearrange("p (h t) -> p h t", h=NH)


def build(nc, a, out):
    with ExitStack() as ctx:
        def sb(name, shape, dt):
            return ctx.enter_context(nc.sbuf_tensor(name, shape, dt))

        def sem(name):
            return ctx.enter_context(nc.semaphore(name))

        def over(name, shape, dt):
            with nc.sbuf_tensor(name, shape, dt) as t:
                return t

        dn_work = over("dn_work", [P, 2 * KD * T], F32)
        act_hi = sb("act_hi", [P, KD, T], F32R)
        act_lo = sb("act_lo", [P, KD, T], F32R)
        h_hi = sb("h_hi", [P, YT + 4, T], F32R)
        adapters = over("adapters", [P, YT + 4, T], F32)
        h_lo = sb("h_lo", [P, YT + 4, T], F32R)
        ring_hi = sb("ring_hi", [P, 2, 1024], F32R)
        ring_lo = sb("ring_lo", [P, 2, 1024], F32R)
        raw = sb("raw", [P, 2, 1024], F32)
        sil = sb("sil", [P, 2, 1024], F32)
        res = sb("res", [P, KD, T], F32)
        cst = sb("cst", [P, C_END], F32)
        shifts = sb("shifts", [P, 2], U32)
        sh8 = shifts[:, 0:1].bitcast(U8)[:, 0:1]
        sh32 = shifts[:, 1:2]
        gidx = sb("gidx", [P, KD + FT0], I32)
        idx_gu = sb("idx_gu", [P, FT0, KD], I32)
        idx_dn = sb("idx_dn", [P, FT0], I32)
        idx_cur = sb("idx_cur", [P, 2, KD], I32)
        zn_dn = sb("zn_dn", [P, 3 * CH0[0] * P // 4], F32)
        ids = sb("ids", [P, NBATCH], I32)
        aid = sb("aid", [1, 3 * NBATCH], I32)
        aidf = sb("aidf", [1, 2 * NBATCH], F32)
        lnw = sb("lnw", [P, KD], F32)
        col = sb("col", [P, 9], F32)
        wr = sb("wr", [P, KD, E], F32)
        wr2 = sb("wr2", [P, KD, 2 * E], F32R)

        ident = cst[:, C_ID:C_ID + P]
        log_T = res[0:2 * E, KD - 1, :]
        work = res[:, :, :].rearrange("p k t -> p (k t)")
        ZW = FT0 * 16
        at = KD * 2 * ZW
        zgp = work[:, 0:at].bitcast(U32)
        nib_gu = work[:, at:at + 256].bitcast(U8)
        z_gu = work[:, at + 256:at + 512].bitcast(U8)
        n_gu = work[:, at + 512:at + 1024].bitcast(BF16)
        qw = [work[:, at + 1024 + 256 * s:at + 1280 + 256 * s].bitcast(U32) for s in range(2)]
        ZD, WD = FT0 * D // 8, CH0[0] * P
        zdp = dn_work[:, 0:ZD].bitcast(U32).rearrange("p (k w) -> p k w", k=FT0)
        sc_dn = dn_work[:, ZD:ZD + FT0 * D].rearrange("p (k n) -> p k n", k=FT0)
        qd = dn_work[:, ZD + FT0 * D:ZD + FT0 * D + 2 * WD].bitcast(U32).rearrange("p (s n) -> p s n", s=2)
        z_dn = zn_dn[:, 0:WD // 4].bitcast(U8)
        n_dn = zn_dn[:, WD // 4:3 * WD // 4].bitcast(BF16)
        warm = zn_dn[:, 0:HALF // 2].bitcast(BF16)
        w0_hi, w0_lo = (t[:, 0:2, :].rearrange("p a (b n) -> p (a b) n", n=D) for t in (h_hi, h_lo))
        a_hi, a_lo = (t[:, 2, 0:512].rearrange("p (k n) -> p k n", n=P) for t in (h_hi, h_lo))
        b_hi, b_lo = (t[:, 2, 512:1024] for t in (h_hi, h_lo))
        hg_hi, hg_lo = (t[:, 3, :] for t in (h_hi, h_lo))
        ab_raw = sil[:, 0, :]
        hg_full = sil[:, 0, :]
        g_exp = raw[:, 0, :]
        g_T = raw[:, 1, :]
        gt = sil[:, 1, :]
        L_log, L_mx, L_eq, L_g1, L_g2 = (gt[:, 64 * i:64 * i + 64] for i in range(5))
        L_mi = gt[:, 320:384].bitcast(U32)
        L_mif, L_idf, L_w = gt[:, 384:448], gt[:, 448:456], gt[:, 456:512]
        idxf = gt[:, 512:640]

        ps = ctx.enter_context(nc.psum_tensor("ps", [P, 8, HALF], F32))

        X_PIECES = [(0, slice(0, HALF)), (0, slice(HALF, T))] + [(k, slice(0, T)) for k in range(1, KD)]
        NX = len(X_PIECES)

        s_x = [sem(f"s_x{i}") for i in range(NX)]
        s_w0 = [sem(f"s_w0{c}") for c in range(2)]
        s_wr, s_b, s_ab, s_cst, s_sh, s_gi, s_id, s_aid, s_ln = (
            sem(n) for n in ("s_wr", "s_b", "s_ab", "s_cst", "s_sh", "s_gi", "s_id", "s_aid", "s_ln"))
        s_xhi, s_xlo, s_whi0, s_wlo0 = (sem(n) for n in ("s_xhi", "s_xlo", "s_whi0", "s_wlo0"))
        s_wrhi, s_wrlo = sem("s_wrhi"), sem("s_wrlo")
        s_log, s_logT, s_logP, s_gate_c, s_exp, s_gex, s_gTp, s_gT = (
            sem(n) for n in ("s_log", "s_logT", "s_logP", "s_gate_c", "s_exp", "s_gex", "s_gTp", "s_gT"))
        s_hA, s_hg, s_hghi, s_hglo = (sem(n) for n in ("s_hA", "s_hg", "s_hghi", "s_hglo"))
        s_y, s_yhi, s_ylo = (sem(n) for n in ("s_y", "s_yhi", "s_ylo"))
        s_idx, s_idc, s_zg, s_aok = (sem(n) for n in ("s_idx", "s_idc", "s_zg", "s_aok"))
        s_td = [sem(f"s_td{c}") for c in range(2)]
        s_warm = sem("s_warm")
        s_v = sem("s_v")
        s_raw = {p: [sem(f"s_raw_{p}{s}") for s in range(2)] for p in ("gu0", "gu1", "d1")}
        s_qw = {p: [sem(f"s_qw_{p}{s}") for s in range(2)] for p in ("gu0", "d0")}
        s_nib, s_zl, s_zh, s_n, s_wf = (sem(n) for n in ("s_nib", "s_zl", "s_zh", "s_n", "s_wf"))
        s_whi = sem("s_whi")
        s_wlo = sem("s_wlo")
        s_gate = sem("s_gate")
        s_ring = sem("s_ring")
        s_silu, s_hm, s_hhi, s_hlo = (sem(n) for n in ("s_silu", "s_hm", "s_hhi", "s_hlo"))
        s_res = sem("s_res")
        s_xr = sem("s_xr")
        s_rhi, s_rlo, s_sq, s_rc, s_rs, s_zs, s_zt, s_nx, s_nhi, s_nlo, s_vv = (
            sem(n) for n in ("s_rhi", "s_rlo", "s_sq", "s_rc", "s_rs", "s_zs", "s_zt", "s_nx", "s_nhi", "s_nlo", "s_vv"))
        s_z = sem("s_z")
        s_ad = [sem(f"s_ad{s}") for s in range(2)]
        s_ahi, s_alo, s_alp = sem("s_ahi"), sem("s_alo"), sem("s_alp")
        s_htwo = sem("s_htwo")
        s_half = sem("s_half")
        s_last = sem("s_last")
        s_out = sem("s_out")

        Q = {"gu0": 0, "d0": FT0, "gu1": FT0 + 8, "d1": FT0 + 8 + FT1}

        def loop(eng, start, end):
            return nc.Fori(start, end, engines=[eng.engine], hint_back_edge=True)

        def adapter_tile(b):
            if isinstance(b, int) and b < 2:
                return YT + 2 * b
            return 2 * b - 4

        def adapter_raw(b, part):
            if isinstance(b, int) and b == 2:
                return sil[:, part:part + 1, :]
            return adapters[:, bass.ds(adapter_tile(b) + part, 1), :]

        def raw_free(eng, q):
            need(eng, s_whi, q - 1)
            need(eng, s_wlo, q - 1)

        block = ctx.enter_context(nc.Block())

        @block.sync
        def _(sp):
            for i, (k, t) in enumerate(X_PIECES):
                sp.dma_start(res[:, k, t], a["xT"][:, k, t]).then_inc(s_x[i], 16)
                if i == 0:
                    sp.dma_start(ab_raw[:, 0:512], a["aT"]).then_inc(s_ab, 16)
                    sp.dma_start(wr[:, :, :], a["wrT"]).then_inc(s_wr, 16)
            for c in range(2):
                sp.dma_start(raw[:, c, :], a["w0T"][:, 1024 * c:1024 * c + 1024]).then_inc(s_w0[c], 16)
            sp.dma_start(ab_raw[:, 512:1024], a["bT"]).then_inc(s_b, 16)

            def load_gu1(i, s):
                raw_free(sp, i + Q["gu1"])
                sp.dma_start(raw[:, 1 - s, :], a["gu1"][bass.ds(i, 1), :, :].rearrange("o p n -> (o p) n")
                             ).then_inc(s_raw["gu1"][s], 16)

            def load_qw(i, s):
                for hp in range(2):
                    sp.dma_start(qw[s][64 * hp:64 * hp + 64, :], a["qw_gu"][bass.ds(i, 1), :, :].rearrange("o r c -> (o r) c")
                                 ).then_inc(s_qw["gu0"][s], 16)

            sp.wait_ge(s_xlo, NX)
            sp.wait_ge(s_xhi, NX)
            for i in range(2):
                load_qw(i, i)
            with loop(sp, 0, (FT0 - 3) // 2) as j:
                for s in range(2):
                    need(sp, s_nib, 2 * j + s + 1)
                    load_qw(2 * j + s + 2, s)
            need(sp, s_nib, FT0 - 2)
            load_qw(FT0 - 1, (FT0 - 1) % 2)

            def load_qd(m, c):
                k0, cnt = CH0[0] * c, CH0[c]
                sp.dma_start(qd[:, c, 0:cnt * P].rearrange("p (k n) -> p k n", n=P),
                             a["qw_dn"][:, bass.ds(m, 1), k0:k0 + cnt, :].rearrange("p o k n -> p (o k) n")
                             ).then_inc(s_qw["d0"][c], 16)

            sp.wait_ge(s_y, KD)
            for c in range(2):
                load_qd(0, c)
            need(sp, s_wf, FT0)
            sp.dma_start(res[:, :, :], a["xT"]).then_inc(s_xr, 16)

            sp.wait_ge(s_aok, 1)
            rows = [sp.value_load(aid[0:1, 2 * NBATCH + b:2 * NBATCH + b + 1], min_val=0, max_val=NBATCH - 1)
                    for b in range(NBATCH)]

            def load_adapter(b, s):
                dst = sil[:, :, :] if b == 2 else adapters[:, bass.ds(adapter_tile(b), 2), :]
                sp.dma_start(dst.rearrange("p a n -> p (a n)"),
                             a["w1T"][bass.ds(rows[b], 1), :, :].rearrange("o p n -> (o p) n")).then_inc(s_ad[s], 16)

            def next_adapter(b, s, value):
                sp.wait_ge(s_ad[s], value)
                load_adapter(b, s)

            def refill_qd(m):
                for c in range(2):
                    need(sp, s_n, FT0 + 2 * m + c - 1)
                    load_qd(m, c)

            refill_qd(1)
            sp.wait_ge(s_ring, FT0)
            for b in range(2):
                load_adapter(b, b)
            sp.wait_ge(s_hhi, FT0)
            sp.wait_ge(s_hlo, FT0)
            next_adapter(2, 0, 16)
            with loop(sp, 2, KD) as m:
                refill_qd(m)
            for i in range(2):
                load_gu1(i, i)

            for b in range(3, NBATCH - 1):
                sp.wait_ge(s_htwo, b - 1)
                next_adapter(b, b % 2, 16 * (b // 2))
            sp.wait_ge(s_ring, Q["gu1"])
            sp.wait_ge(s_z, 1)
            next_adapter(NBATCH - 1, 1, 16 * (NBATCH // 2 - 1))

            with loop(sp, 1, FT1 // 2) as j:
                for s in range(2):
                    load_gu1(2 * j + s, s)
            with loop(sp, 0, KD) as m:
                for c in range(2):
                    n = CH1[c] * P
                    raw_free(sp, 2 * m + c + Q["d1"])
                    sp.dma_start(raw[:, 1 - c, 0:n], a["d1"][bass.ds(m, 1), :, n * c:n * c + n].rearrange("o p n -> (o p) n")
                                 ).then_inc(s_raw["d1"][c], 16)
            with loop(sp, 0, KD - 1) as m:
                sp.wait_ge(s_res, m + KD + 2)
                sp.dma_start(out[bass.ds(m, 1), :, :].rearrange("o p t -> (o p) t"), res[:, bass.ds(m, 1), :].rearrange(
                    "p o t -> p (o t)")).then_inc(s_out, 16)
            for hf in range(NH):
                sp.wait_ge(s_last, hf + 1)
                t = slice(HALF * hf, HALF * hf + HALF)
                sp.dma_start(out[KD - 1, :, t], res[:, KD - 1, t]).then_inc(s_out, 16)
            sp.wait_ge(s_out, 16 * (KD + 1))

        @block.gpsimd
        def _(pool):
            pool.dma_start(cst[:, :], a["cst"]).then_inc(s_cst, 16)
            pool.dma_start(gidx[:, :], a["gidx"]).then_inc(s_gi, 16)
            pool.dma_start(ids[:, :], a["ids"].partition_broadcast(P)).then_inc(s_id, 16)
            pool.dma_start(aid[:, 0:NBATCH], a["aids"].partition_broadcast(1)).then_inc(s_aid, 16)
            pool.dma_start(lnw[:, :], a["lnw"]).then_inc(s_ln, 16)
            pool.dma_start(shifts[:, :], a["shifts"]).then_inc(s_sh, 16)

            def gather(dst, table, index, done):
                pool.indirect_dma_start(dst, None, table, bass.IndirectOffsetOnAxis(ap=index, axis=0)).then_inc(done, 16)

            pool.wait_ge(s_idx, 2)
            pool.wait_ge(s_xlo, NX)
            pool.wait_ge(s_xhi, NX)
            for k in range(KD):
                gather(zgp[:, 2 * ZW * k:2 * ZW * (k + 1)], a["qz_gu"], idx_gu[:, 0, k:k + 1], s_zg)

            def scales_gu(i, s):
                raw_free(pool, i)
                pool.tensor_copy(idx_cur[:, s, 0:KD], idx_gu[:, bass.ds(i, 1), :].rearrange("p o k -> p (o k)")).then_inc(s_idc, 1)
                pool.drain()
                for k in range(KD):
                    gather(raw[:, s, 256 * k:256 * k + 256], a["sc_gu"], idx_cur[:, s, k:k + 1], s_raw["gu0"][s])

            pool.wait_ge(s_hg, 1)
            for i in range(2):
                scales_gu(i, i)
            with loop(pool, 1, FT0 // 2) as j:
                for s in range(2):
                    scales_gu(2 * j + s, s)
            scales_gu(FT0 - 1, 0)
            pool.wait_ge(s_y, KD)
            for i in range(FT0):
                c = i // CH0[0]
                gather(zdp[:, i, :], a["qz_dn"], idx_dn[:, i:i + 1], s_td[c])
                gather(sc_dn[:, i, :], a["sc_dn"], idx_dn[:, i:i + 1], s_td[c])

            def adapter_lo(b):
                t = bass.ds(adapter_tile(b) + 1, 1)
                need(pool, s_ahi, 2 * b + 2)
                pool.tensor_tensor(h_lo[:, t, :], adapter_raw(b, 1), h_hi[:, t, :].bitcast(F32), ALU.subtract).then_inc(s_alp, 1)

            for b in range(3):
                adapter_lo(b)
            with loop(pool, 3, NBATCH) as b:
                adapter_lo(b)

        @block.scalar
        def _(act):
            def hi(dst, src, done):
                act.activation(dst, src, ACT.Copy).then_inc(done, 1)

            for i, (k, t) in enumerate(X_PIECES):
                act.wait_ge(s_x[i], 16)
                hi(act_hi[:, k, t], res[:, k, t], s_xhi)
                if i == 0:
                    act.wait_ge(s_ab, 16)
                    hi(h_hi[:, 2, 0:512], ab_raw[:, 0:512], s_whi0)
                    act.wait_ge(s_wr, 16)
                    hi(wr2[:, :, 0:E], wr[:, :, :], s_wrhi)
            for c in range(2):
                act.wait_ge(s_w0[c], 16)
                hi(h_hi[:, c, :], raw[:, c, :], s_whi0)
            act.wait_ge(s_b, 16)
            hi(h_hi[:, 2, 512:1024], ab_raw[:, 512:1024], s_whi0)
            act.wait_ge(s_log, 1)
            act.activation(log_T.rearrange("e (h t) -> e h t", h=NH), ps[0:2 * E, 2:4, :], ACT.Copy).then_inc(s_logT, 1)
            act.wait_ge(s_gate_c, 1)
            act.activation(L_w[:, 8:16], L_w[:, 0:8], ACT.Exp).then_inc(s_exp, 1)
            act.wait_ge(s_gTp, 1)
            act.activation(halves(g_T), ps[:, 2:4, :], ACT.Copy).then_inc(s_gT, 1)
            act.wait_ge(s_hg, 1)
            hi(hg_hi, hg_full, s_hghi)

            def y_split(m, b):
                act.wait_ge(s_y, m + 1)
                hi(halves(h_hi[:, YT + m, :]), ps[:, b:b + 2, :], s_yhi)

            def w_hi(q, s, width, loaded, value):
                need(act, loaded, value)
                need(act, s_ring, q - 1)
                hi(ring_hi[:, s, 0:width], raw[:, s, 0:width], s_whi)

            def w_hi_gu(ph, i, s):
                if ph == "gu0":
                    w_hi(i, s, 1024, s_wf, i + 1)
                else:
                    w_hi(i + Q[ph], 1 - s, 1024, s_raw[ph][s], (i - s) * 8 + 16)

            def w_hi_dn(ph, m, c):
                if ph == "d0":
                    w_hi(2 * m + c + Q[ph], 1 - c, CH0[c] * P, s_wf, FT0 + 2 * m + c + 1)
                else:
                    w_hi(2 * m + c + Q[ph], 1 - c, CH1[c] * P, s_raw[ph][c], 16 * m + 16)

            def silu(i, s, base):
                need(act, s_gate, i + base + 1)
                need(act, s_hlo, i + base - 1)
                act.activation(halves(sil[:, s, :]), ps[:, 4 * s:4 * s + 2, :], ACT.Silu).then_inc(s_silu, 1)

            def h_split(i, s, base):
                need(act, s_hm, i + base + 1)
                hi(h_hi[:, bass.ds(i, 1), :].rearrange("p o t -> p (o t)"), sil[:, s, :], s_hhi)

            def gu_step(i, s, base, fill):
                silu(i, s, base)
                fill()
                h_split(i, s, base)

            y_split(0, 0)
            w_hi_gu("gu0", 0, 0)
            y_split(1, 4)
            y_split(2, 6)
            y_split(3, 2)
            w_hi_gu("gu0", 1, 1)
            for i in range(2):
                gu_step(i, i, 0, lambda: w_hi_gu("gu0", i + 2, i))
            with loop(act, 1, FT0 // 2 - 1) as j:
                for s in range(2):
                    i = 2 * j + s
                    gu_step(i, s, 0, lambda: w_hi_gu("gu0", i + 2, s))
            gu_step(FT0 - 3, 0, 0, lambda: w_hi_gu("gu0", FT0 - 1, 0))
            for c in range(2):
                gu_step(FT0 - 2 + c, 1 - c, 0, lambda: w_hi_dn("d0", 0, c))

            def adapter_hi(b, s, value, part):
                need(act, s_ad[s], value)
                t = bass.ds(adapter_tile(b) + part, 1)
                hi(h_hi[:, t, :], adapter_raw(b, part), s_ahi)

            with loop(act, 1, KD) as m:
                for c in range(2):
                    w_hi_dn("d0", m, c)
            for b in range(2):
                for part in range(2):
                    adapter_hi(b, b, 16, part)
            act.wait_ge(s_wf, Q["gu1"])
            for m in range(KD - 1):
                need(act, s_res, m + 1)
                hi(act_hi[:, m, :], res[:, m, :], s_rhi)
            act.wait_ge(s_ln, 16)
            act.activation(col[:, 8:9], lnw[:, 0:1], ACT.Sqrt)
            for hf in range(NH):
                need(act, s_res, KD + hf)
                t = slice(HALF * hf, HALF * hf + HALF)
                hi(act_hi[:, KD - 1, t], res[:, KD - 1, t], s_rhi)
                if hf == 0:
                    act.wait_ge(s_htwo, 1)
                    for part in range(2):
                        adapter_hi(2, 0, 32, part)

            def batch_z(b, s):
                need(act, s_z, b + 1)
                act.activation(sil[:, s, 0:D], ps[:, 4 + s, :], ACT.Square, accum_out=col[:, s:s + 1]).then_inc(s_sq, 1)

            def batch_n(b, s):
                need(act, s_nx, b + 1)
                hi(act_hi[:, :, bass.ds(b * SEQ, SEQ)], sil[:, s, D:2 * D].rearrange("p (k t) -> p k t", k=KD), s_nhi)

            def batch_r(b, s):
                need(act, s_rc, b + 1)
                act.activation(col[:, 4 + s:5 + s], col[:, 2 + s:3 + s], ACT.Sqrt).then_inc(s_rs, 1)

            def batch_step(b, s, ahead=lambda part: None):
                batch_z(b, s)
                ahead(0)
                batch_r(b, s)
                batch_n(b - 1, 1 - s)
                ahead(1)

            act.wait_ge(s_alo, 3)
            act.wait_ge(s_alp, 3)
            batch_z(0, 0)
            batch_r(0, 0)
            for part in range(2):
                adapter_hi(3, 1, 32, part)
            with loop(act, 0, 2) as j:
                for s in range(2):
                    batch_step(2 * j + s + 1, 1 - s, lambda part: adapter_hi(2 * j + s + 4, s, 16 * j + 48, part))
            batch_step(5, 1, lambda part: w_hi_gu("gu1", 0, 0) if part == 0 else None)
            batch_step(6, 0)
            batch_step(7, 1)
            batch_n(NBATCH - 1, 1)
            w_hi_gu("gu1", 1, 1)

            with loop(act, 0, FT1 // 2 - 1) as j:
                for s in range(2):
                    i = 2 * j + s
                    gu_step(i, s, FT0, lambda: w_hi_gu("gu1", i + 2, s))
            for c in range(2):
                gu_step(FT1 - 2 + c, c, FT0, lambda: w_hi_dn("d1", 0, c))
            with loop(act, 1, KD) as m:
                for c in range(2):
                    w_hi_dn("d1", m, c)

        @block.vector
        def _(dve):
            done = [0]

            def own(ins):
                done[0] += 1
                ins.then_inc(s_v, 1)
                dve.wait_ge(s_v, done[0])

            def lo(dst, src, hi_part, done_sem):
                dve.tensor_tensor(dst, src, hi_part.bitcast(F32), ALU.subtract).then_inc(done_sem, 1)

            dve.memset(warm, 0.0).then_inc(s_warm, 1)
            for i, (k, t) in enumerate(X_PIECES):
                dve.wait_ge(s_xhi, i + 1)
                lo(act_lo[:, k, t], res[:, k, t], act_hi[:, k, t], s_xlo)
                if i == 0:
                    dve.wait_ge(s_whi0, 1)
                    lo(h_lo[:, 2, 0:512], ab_raw[:, 0:512], h_hi[:, 2, 0:512], s_wlo0)
                    dve.wait_ge(s_wrhi, 1)
                    lo(wr2[:, :, E:2 * E], wr[:, :, :], wr2[:, :, 0:E], s_wrlo)
            for c in range(2):
                dve.wait_ge(s_whi0, 2 + c)
                lo(h_lo[:, c, :], raw[:, c, :], h_hi[:, c, :], s_wlo0)
            dve.wait_ge(s_whi0, 4)
            lo(h_lo[:, 2, 512:1024], ab_raw[:, 512:1024], h_hi[:, 2, 512:1024], s_wlo0)

            dve.wait_ge(s_gi, 16)
            dve.wait_ge(s_cst, 16)
            g_f, g_n = idxf[:, 0:15], idxf[:, 16:31]
            own(dve.tensor_copy(g_f, gidx[:, :]))
            for lo_c, hi_c, n in ((0, KD, G_GU), (KD, KD + FT0, G_DN)):
                own(dve.tensor_scalar(g_n[:, lo_c:hi_c], g_f[:, lo_c:hi_c], 0.0, float(n), ALU.is_lt, ALU.mult))
                own(dve.tensor_tensor(g_n[:, lo_c:hi_c], g_f[:, lo_c:hi_c], g_n[:, lo_c:hi_c], ALU.add))
                own(dve.tensor_scalar(g_n[:, lo_c:hi_c], g_n[:, lo_c:hi_c], 0.0, float(n - 1), ALU.max, ALU.min))
            dve.tensor_tensor(idx_gu[:, :, :], g_n[:, 0:KD].unsqueeze(1).to_broadcast([P, FT0, KD]),
                              cst[:, C_OGU:C_END].rearrange("p (i k) -> p i k", k=KD), ALU.add).then_inc(s_idx, 1)
            dve.tensor_copy(idx_dn[:, :], g_n[:, KD:KD + FT0]).then_inc(s_idx, 1)
            dve.wait_ge(s_aid, 16)
            a_f, a_n = aidf[:, 0:NBATCH], aidf[:, NBATCH:2 * NBATCH]
            own(dve.tensor_copy(a_f, aid[:, 0:NBATCH]))
            own(dve.tensor_scalar(a_n, a_f, 0.0, float(NBATCH), ALU.is_lt, ALU.mult))
            own(dve.tensor_tensor(a_n, a_f, a_n, ALU.add))
            dve.tensor_scalar(aid[:, 2 * NBATCH:3 * NBATCH], a_n, 0.0, float(NBATCH - 1), ALU.max, ALU.min).then_inc(s_aok, 1)

            def g3(ap):
                return ap.rearrange("p (b e) -> p b e", e=E)

            iota = cst[:, C_IOTA:C_IOTA + E].unsqueeze(1).to_broadcast([P, NBATCH, E])

            def per_batch(ap):
                return ap.unsqueeze(2).to_broadcast([P, NBATCH, E])

            dve.wait_ge(s_id, 16)
            own(dve.tensor_copy(L_idf, ids[:, :]))
            own(dve.tensor_tensor(g3(L_eq), per_batch(L_idf), iota, ALU.is_equal))
            dve.wait_ge(s_logP, 1)
            logs = ps[:, 2, 0:NBATCH * 2 * E].rearrange("p (b i e) -> p b i e", i=2, e=E)
            own(dve.tensor_copy(g3(L_g1), logs[:, :, 1, :]))
            own(dve.tensor_tensor(g3(L_log), logs[:, :, 0, :], g3(L_g1), ALU.add))
            own(dve.scalar_tensor_tensor(out=L_log, in0=L_eq, scalar=LANG_BIAS, in1=L_log, op0=ALU.mult, op1=ALU.add))
            for b in range(NBATCH):
                ins = dve.max(L_mx[:, 8 * b:8 * b + 8], L_log[:, 8 * b:8 * b + 8])
            own(ins)
            for b in range(NBATCH):
                ins = dve.max_index(L_mi[:, 8 * b:8 * b + 8], L_mx[:, 8 * b:8 * b + 8], L_log[:, 8 * b:8 * b + 8])
            own(ins)
            dve.tensor_tensor(L_w[:, 0:8], g3(L_mx)[:, :, 1], g3(L_mx)[:, :, 0], ALU.subtract).then_inc(s_gate_c, 1)
            own(dve.tensor_copy(L_mif, L_mi))
            own(dve.tensor_tensor(g3(L_g1), per_batch(g3(L_mif)[:, :, 0]), iota, ALU.is_equal))
            own(dve.tensor_tensor(g3(L_g2), per_batch(g3(L_mif)[:, :, 1]), iota, ALU.is_equal))
            dve.wait_ge(s_exp, 1)
            own(dve.tensor_scalar(L_w[:, 16:24], L_w[:, 8:16], 1.0, None, ALU.add))
            own(dve.reciprocal(L_w[:, 24:32], L_w[:, 16:24]))
            own(dve.tensor_scalar(L_w[:, 32:40], L_w[:, 24:32], SCALING, None, ALU.mult))
            own(dve.tensor_tensor(L_w[:, 40:48], L_w[:, 32:40], L_w[:, 8:16], ALU.mult))
            own(dve.tensor_tensor(g3(L_g1), g3(L_g1), per_batch(L_w[:, 32:40]), ALU.mult))
            own(dve.tensor_tensor(g3(L_g2), g3(L_g2), per_batch(L_w[:, 40:48]), ALU.mult))
            own(dve.tensor_tensor(L_g1, L_g1, L_g2, ALU.add))
            dve.wait_ge(s_wlo0, 4)
            dve.tensor_copy(g_exp.rearrange("p (g r) -> p g r", r=R),
                            L_g1.unsqueeze(2).to_broadcast([P, NBATCH * E, R])).then_inc(s_gex, 1)
            dve.wait_ge(s_gT, 1)
            dve.wait_ge(s_hA, 1)
            dve.tensor_tensor(halves(hg_full), ps[:, 6:8, :], halves(g_T), ALU.mult).then_inc(s_hg, 1)
            dve.wait_ge(s_hghi, 1)
            lo(hg_lo, hg_full, hg_hi, s_hglo)

            def y_split(m, b):
                dve.wait_ge(s_yhi, m + 1)
                lo(halves(h_lo[:, YT + m, :]), ps[:, b:b + 2, :], halves(h_hi[:, YT + m, :]), s_ylo)

            def w_lo(q, s, width):
                need(dve, s_whi, q + 1)
                lo(ring_lo[:, s, 0:width], raw[:, s, 0:width], ring_hi[:, s, 0:width], s_wlo)

            dve.wait_ge(s_sh, 16)
            dve.wait_ge(s_zg, 16 * KD)
            zg8 = zgp.bitcast(U8).rearrange("p (g w) -> p g w", g=2 * KD)
            z3 = z_gu.rearrange("p (g w e) -> p g w e", g=2 * KD, e=2)

            def dequant_gu(i, s):
                need(dve, s_qw["gu0"][s], (i - s) * 16 + 32)
                need(dve, s_n, i)
                words = qw[s].bitcast(U8).rearrange("p (c j) -> p j c", j=4)
                dve.tensor_scalar(nib_gu.rearrange("p (j c) -> p j c", j=4), words, sh8, 15,
                                  ALU.logical_shift_right, ALU.bitwise_and).then_inc(s_nib, 1)
                zw = zg8[:, :, bass.ds(i * 64, 64)]
                dve.tensor_scalar(z3[:, :, :, 0], zw, 15, None, ALU.bitwise_and).then_inc(s_zl, 1)
                dve.tensor_scalar(z3[:, :, :, 1], zw, 4, None, ALU.logical_shift_right).then_inc(s_zh, 1)
                need(dve, s_nib, i + 1)
                need(dve, s_zl, i + 1)
                need(dve, s_zh, i + 1)
                need(dve, s_wf, i)
                dve.scalar_tensor_tensor(out=n_gu, in0=nib_gu, scalar=1.0, in1=z_gu, op0=ALU.subtract,
                                         op1=ALU.subtract).then_inc(s_n, 1)
                need(dve, s_n, i + 1)
                need(dve, s_raw["gu0"][s], (i - s) * 32 + 64)
                dve.tensor_tensor(raw[:, s, :], raw[:, s, :], n_gu, ALU.mult).then_inc(s_wf, 1)

            def dequant_dn(m, c):
                if m == 0:
                    dve.wait_ge(s_td[c], 2 * 16 * CH0[c])
                k0, cnt = CH0[0] * c, CH0[c]
                e = 2 * m + c + FT0
                need(dve, s_qw["d0"][c], 16 * m + 16)
                q = qd[:, c, 0:cnt * P]
                dve.tensor_scalar(q, q, sh32, 15, ALU.logical_shift_right, ALU.bitwise_and).then_inc(s_nib, 1)
                zw = zdp[:, k0:k0 + cnt, :].bitcast(U8)[:, :, bass.ds(m * 64, 64)]
                z4 = z_dn[:, 0:cnt * P].rearrange("p (k w e) -> p k w e", k=cnt, e=2)
                need(dve, s_n, e)
                dve.tensor_scalar(z4[:, :, :, 0], zw, 15, None, ALU.bitwise_and).then_inc(s_zl, 1)
                dve.tensor_scalar(z4[:, :, :, 1], zw, 4, None, ALU.logical_shift_right).then_inc(s_zh, 1)
                need(dve, s_nib, e + 1)
                need(dve, s_zl, e + 1)
                need(dve, s_zh, e + 1)
                need(dve, s_wf, e)
                dve.scalar_tensor_tensor(out=n_dn[:, 0:cnt * P], in0=q, scalar=1.0, in1=z_dn[:, 0:cnt * P],
                                         op0=ALU.subtract, op1=ALU.subtract).then_inc(s_n, 1)
                need(dve, s_n, e + 1)
                raw_free(dve, 2 * m + c + Q["d0"])
                dve.tensor_tensor(raw[:, 1 - c, 0:cnt * P].rearrange("p (k n) -> p k n", n=P), sc_dn[:, k0:k0 + cnt, P * m:P * m + P],
                                  n_dn[:, 0:cnt * P].rearrange("p (k n) -> p k n", n=P), ALU.mult).then_inc(s_wf, 1)

            def gu_step(i, s, base, nbase, fill):
                need(dve, s_silu, i + base + 1)
                need(dve, s_ring, i + nbase + 1)
                dve.tensor_tensor(halves(sil[:, s, :]), halves(sil[:, s, :]), ps[:, 4 * s + 2:4 * s + 4, :],
                                  ALU.mult).then_inc(s_hm, 1)
                fill()
                need(dve, s_hhi, i + base + 1)
                t = bass.ds(i, 1)
                lo(h_lo[:, t, :].rearrange("p o t -> p (o t)"), sil[:, s, :],
                   h_hi[:, t, :].rearrange("p o t -> p (o t)"), s_hlo)

            def w_lo_dn(m, c):
                w_lo(2 * m + c + Q["d0"], 1 - c, CH0[c] * P)

            dequant_gu(0, 0)
            y_split(0, 0)
            w_lo(0, 0, 1024)
            y_split(1, 4)
            y_split(2, 6)
            y_split(3, 2)
            dequant_gu(1, 1)
            w_lo(1, 1, 1024)
            dequant_gu(2, 0)
            for i in range(2):
                gu_step(i, i, 0, Q["gu0"], lambda: w_lo(i + 2, i, 1024))
                dequant_gu(i + 3, 1 - i)
            with loop(dve, 1, FT0 // 2 - 1) as j:
                for s in range(2):
                    i = 2 * j + s
                    gu_step(i, s, 0, Q["gu0"], lambda: w_lo(i + 2, s, 1024))
                    dequant_gu(i + 3, 1 - s)
            gu_step(FT0 - 3, 0, 0, Q["gu0"], lambda: w_lo(FT0 - 1, 0, 1024))
            for e in range(2):
                dequant_dn(0, e)
                gu_step(FT0 - 2 + e, 1 - e, 0, Q["gu0"], lambda: w_lo_dn(0, e))
            dequant_dn(1, 0)

            def adapter_lo(b):
                need(dve, s_ahi, 2 * b + 1)
                t = bass.ds(adapter_tile(b), 1)
                lo(h_lo[:, t, :], adapter_raw(b, 0), h_hi[:, t, :], s_alo)

            def r_lo(m, t):
                need(dve, s_rhi, m + 1 + t.start // HALF)
                lo(act_lo[:, m, t], res[:, m, t], act_hi[:, m, t], s_rlo)

            def add_res(m, bank, n_last):
                need(dve, s_ring, n_last + 1)
                t = res[:, bass.ds(m, 1), :].rearrange("p o (h t) -> p (o h) t", h=NH)
                dve.tensor_tensor(t, ps[:, bank, :], t, ALU.add).then_inc(s_res, 1)

            dve.wait_ge(s_xr, 16)
            for m in range(1, KD):
                w_lo_dn(m, 0)
                dequant_dn(m, 1)
                w_lo_dn(m, 1)
                if m < KD - 1:
                    dequant_dn(m + 1, 0)
                add_res(m - 1, slice((2 + 2 * m) % 8, (2 + 2 * m) % 8 + 2), Q["d0"] + 2 * m - 1)
            dve.wait_ge(s_wf, Q["gu1"])
            for m in range(KD - 1):
                r_lo(m, slice(0, T))
            for b in range(2):
                adapter_lo(b)
            for hf in range(NH):
                dve.wait_ge(*((s_half, 1) if hf == 0 else (s_ring, Q["gu1"])))
                t = slice(HALF * hf, HALF * hf + HALF)
                dve.tensor_tensor(res[:, KD - 1, t], ps[:, 2 + hf, :], res[:, KD - 1, t], ALU.add).then_inc(s_res, 1)
                r_lo(KD - 1, t)
                if hf == 0:
                    adapter_lo(2)

            def var(b, s):
                need(dve, s_sq, b + 1)
                dve.tensor_scalar(col[:, 6 + s:7 + s], col[:, s:s + 1], 1.0 / D, EPS, ALU.mult, ALU.add).then_inc(s_vv, 1)
                need(dve, s_vv, b + 1)
                dve.reciprocal(col[:, 2 + s:3 + s], col[:, 6 + s:7 + s]).then_inc(s_rc, 1)

            def norm(b, s):
                need(dve, s_rs, b + 1)
                dve.tensor_scalar(sil[:, s, 0:D], ps[:, 4 + s, :], col[:, 4 + s:5 + s], None, ALU.mult).then_inc(s_zs, 1)

            def weigh(b, s):
                need(dve, s_zt, b + 1)
                dve.tensor_tensor(sil[:, s, D:2 * D].rearrange("p (k t) -> p k t", k=KD),
                                  ps[:, 6 + s, :].rearrange("p (k t) -> p k t", k=KD),
                                  lnw[:, :].unsqueeze(2).to_broadcast([P, KD, SEQ]), ALU.mult).then_inc(s_nx, 1)

            def n_lo(b, s):
                need(dve, s_nhi, b + 1)
                t = bass.ds(b * SEQ, SEQ)
                lo(act_lo[:, :, t], sil[:, s, D:2 * D].rearrange("p (k t) -> p k t", k=KD), act_hi[:, :, t], s_nlo)
                need(dve, s_nlo, b + 1)

            dve.wait_ge(s_ln, 16)

            def batch_step(b, s, ahead=lambda: None):
                var(b, s)
                weigh(b - 1, 1 - s)
                norm(b, s)
                ahead()
                n_lo(b - 1, 1 - s)

            var(0, 0)
            norm(0, 0)
            adapter_lo(3)
            with loop(dve, 0, 2) as j:
                for s in range(2):
                    batch_step(2 * j + s + 1, 1 - s, lambda: adapter_lo(2 * j + s + 4))
            batch_step(5, 1)
            batch_step(6, 0, lambda: w_lo(Q["gu1"], 1, 1024))
            batch_step(7, 1)
            weigh(NBATCH - 1, 1)
            n_lo(NBATCH - 1, 1)
            w_lo(1 + Q["gu1"], 0, 1024)

            def gu1_fill(i, s):
                w_lo(i + Q["gu1"], 1 - s, 1024)

            def d1_fill(m, c):
                w_lo(2 * m + c + Q["d1"], 1 - c, CH1[c] * P)

            with loop(dve, 0, FT1 // 2 - 1) as j:
                for s in range(2):
                    gu_step(2 * j + s, s, FT0, Q["gu1"], lambda: gu1_fill(2 * j + s + 2, s))
            for c in range(2):
                gu_step(FT1 - 2 + c, c, FT0, Q["gu1"], lambda: d1_fill(0, c))
            for m in range(KD):
                if m < KD - 1:
                    for c in range(2):
                        d1_fill(m + 1, c)
                    add_res(m, slice(2 * m, 2 * m + 2), Q["d1"] + 2 * m + 1)
            for hf in range(NH):
                dve.wait_ge(*((s_half, 2) if hf == 0 else (s_ring, Q["d1"] + 2 * KD)))
                t = slice(HALF * hf, HALF * hf + HALF)
                dve.tensor_tensor(res[:, KD - 1, t], ps[:, 2 * (KD - 1) + hf, :], res[:, KD - 1, t], ALU.add).then_inc(s_last, 1)

        @block.tensor
        def _(pe):
            def mm3(bank, w_hi, w_lo, v_hi, v_lo, first, last, hfs=range(NH)):
                for hf in hfs:
                    t = slice(HALF * hf, HALF * hf + HALF)
                    pe.matmul(ps[:, bank + hf, :], w_hi, v_hi[:, t], start=first, stop=False)
                    pe.matmul(ps[:, bank + hf, :], w_hi, v_lo[:, t], start=False, stop=False)
                for hf in hfs:
                    t = slice(HALF * hf, HALF * hf + HALF)
                    ins = pe.matmul(ps[:, bank + hf, :], w_lo, v_hi[:, t], start=False, stop=last)
                return ins

            pe.wait_ge(s_warm, 1)
            for _ in range(11):
                pe.matmul(ps[:, 0, :], warm[:, 0:P], warm, start=True, stop=True)

            for i, (k, t) in enumerate(X_PIECES):
                pe.wait_ge(s_xhi, i + 1)
                pe.wait_ge(s_xlo, i + 1)
                if i == 0:
                    pe.wait_ge(s_wlo0, 1)
                    pe.wait_ge(s_wrlo, 1)
                hfs = range(t.start // HALF, t.stop // HALF)
                ins = mm3(6, a_hi[:, k, :], a_lo[:, k, :], act_hi[:, k, :], act_lo[:, k, :], k == 0, k == KD - 1, hfs)
                for hf in hfs:
                    th = slice(HALF * hf, HALF * hf + HALF)
                    pe.matmul(ps[0:2 * E, 2 + hf, :], wr2[:, k, :], act_hi[:, k, th], start=(k == 0), stop=False)
                    log = pe.matmul(ps[0:2 * E, 2 + hf, :], wr2[:, k, :], act_lo[:, k, th], start=False, stop=(k == KD - 1))
            ins.then_inc(s_hA, 1)
            log.then_inc(s_log, 1)

            def base(m, bank, ks=range(KD)):
                for k in ks:
                    c = slice(P * m, P * m + P)
                    mm3(bank, w0_hi[:, k, c], w0_lo[:, k, c], act_hi[:, k, :], act_lo[:, k, :], k == 0, False)

            def lora(m, bank):
                c = slice(P * m, P * m + P)
                mm3(bank, b_hi[:, c], b_lo[:, c], hg_hi, hg_lo, False, True).then_inc(s_y, 1)

            pe.wait_ge(s_wlo0, 3)
            base(0, 0, range(0, 1))
            pe.wait_ge(s_cst, 16)
            pe.wait_ge(s_logT, 1)
            for b in range(NBATCH):
                ins = pe.transpose(ps[:, 2, 2 * E * b:2 * E * b + 2 * E], log_T[:, P * b:P * b + P], ident[0:2 * E, 0:2 * E])
            ins.then_inc(s_logP, 1)
            base(0, 0, range(1, KD))
            base(1, 4, range(0, 2))
            pe.wait_ge(s_gex, 1)
            for b in range(NBATCH):
                ins = pe.transpose(ps[:, 2 + b // 4, P * (b % 4):P * (b % 4) + P], g_exp[:, P * b:P * b + P], ident)
            ins.then_inc(s_gTp, 1)
            base(1, 4, range(2, KD))
            pe.wait_ge(s_hg, 1)
            base(2, 6)
            pe.wait_ge(s_hglo, 1)
            lora(0, 0)
            lora(1, 4)
            lora(2, 6)
            base(3, 2)
            lora(3, 2)

            def weights_ready(q):
                need(pe, s_whi, q + 1)
                need(pe, s_wlo, q + 1)

            def gate_up(q, s, i, slot, act_at, k_done=None):
                weights_ready(q)
                need(pe, s_hm, i - 1)
                for g in range(2):
                    for k in range(KD):
                        c = slice(256 * k + P * g, 256 * k + P * g + P)
                        if k_done is not None and g == 0:
                            pe.wait_ge(k_done, k + 1)
                        ins = mm3(4 * s + 2 * g, ring_hi[:, slot, c], ring_lo[:, slot, c],
                                  act_at[0][:, k, :], act_at[1][:, k, :], k == 0, k == KD - 1)
                    ins.then_inc(s_ring if g else s_gate, 1)

            y_at = (h_hi[:, YT:YT + KD, :], h_lo[:, YT:YT + KD, :])
            gate_up(0, 0, 0, 0, y_at, s_ylo)
            gate_up(1, 1, 1, 1, y_at)
            with loop(pe, 1, FT0 // 2) as j:
                for s in range(2):
                    gate_up(2 * j + s, s, 2 * j + s, s, y_at)
            gate_up(FT0 - 1, 0, FT0 - 1, 0, y_at)

            def down(m, q0, chunks, bank, h_done):
                for c in range(2):
                    weights_ready(q0 + 2 * m + c)
                    for k in range(chunks[c]):
                        i = chunks[0] * c + k
                        if m == 0:
                            pe.wait_ge(s_hhi, h_done + i + 1)
                            pe.wait_ge(s_hlo, h_done + i + 1)
                        w = slice(P * k, P * k + P)
                        ins = mm3(bank, ring_hi[:, 1 - c, w], ring_lo[:, 1 - c, w], h_hi[:, i, :], h_lo[:, i, :],
                                  i == 0, i == sum(chunks) - 1)
                    ins.then_inc(s_ring, 1)

            def down_halves(m, q0, chunks, bank, pair=None):
                for hf in range(NH):
                    for i in range(sum(chunks)):
                        c, k = divmod(i, chunks[0])
                        if hf == 0 and k == 0:
                            weights_ready(q0 + 2 * m + c)
                        w = slice(P * k, P * k + P)
                        ins = mm3(bank, ring_hi[:, 1 - c, w], ring_lo[:, 1 - c, w], h_hi[:, i, :], h_lo[:, i, :],
                                  i == 0, i == sum(chunks) - 1, [hf])
                        if pair is not None and hf == NH - 1 and i % 2:
                            ins.then_inc(pair, 1)
                    ins.then_inc(*((s_half, 1) if hf == 0 else (s_ring, 2)))

            pe.wait_ge(s_hm, FT0 - 1)
            for m in range(KD - 1):
                down(m, Q["d0"], CH0, (4 + 2 * m) % 8, 0)
            down_halves(KD - 1, Q["d0"], CH0, 2, s_htwo)

            def z_product(b, s):
                need(pe, s_rhi, KD + b // 4)
                need(pe, s_rlo, KD + b // 4)
                need(pe, s_ahi, b + 1)
                need(pe, s_alo, b + 1)
                need(pe, s_alp, b + 1)
                need(pe, s_zs, b - 1)
                at_b = adapter_tile(b)
                w_hi, w_lo = (t[:, at_b:at_b + 2, :].rearrange("p a (c n) -> p (a c) n", n=D) for t in (h_hi, h_lo))
                t = slice(SEQ * b, SEQ * b + SEQ)
                for k in range(KD):
                    pe.matmul(ps[:, 4 + s, :], act_hi[:, k, t], w_hi[:, k, :], start=(k == 0), stop=False)
                    pe.matmul(ps[:, 4 + s, :], act_hi[:, k, t], w_lo[:, k, :], start=False, stop=False)
                    ins = pe.matmul(ps[:, 4 + s, :], act_lo[:, k, t], w_hi[:, k, :], start=False, stop=(k == KD - 1))
                ins.then_inc(s_z, 1)

            def turn(b, s):
                need(pe, s_zs, b + 1)
                need(pe, s_nx, b - 1)
                for k in range(KD):
                    ins = pe.transpose(ps[:, 6 + s, P * k:P * k + P], sil[:, s, P * k:P * k + P], ident)
                ins.then_inc(s_zt, 1)

            z_product(0, 0)
            for b in range(1, NBATCH):
                z_product(b, b % 2)
                turn(b - 1, 1 - b % 2)

            z_at = (act_hi, act_lo)
            weights_ready(Q["gu1"])
            for hf in range(NH):
                pe.wait_ge(s_nhi, (hf + 1) * NBATCH // NH)
                pe.wait_ge(s_nlo, (hf + 1) * NBATCH // NH)
                for g in range(2):
                    for k in range(KD):
                        c = slice(256 * k + P * g, 256 * k + P * g + P)
                        ins = mm3(2 * g, ring_hi[:, 1, c], ring_lo[:, 1, c], act_hi[:, k, :], act_lo[:, k, :],
                                  k == 0, k == KD - 1, [hf])
                    if hf == 0 and g == 0:
                        turn(NBATCH - 1, 1)
                    if hf == NH - 1:
                        ins.then_inc(s_ring if g else s_gate, 1)
            gate_up(1 + Q["gu1"], 1, 1 + FT0, 0, z_at)
            with loop(pe, 1, FT1 // 2) as j:
                for s in range(2):
                    gate_up(2 * j + s + Q["gu1"], s, 2 * j + s + FT0, 1 - s, z_at)
            pe.wait_ge(s_hm, FT0 + FT1 - 1)
            for m in range(KD - 1):
                down(m, Q["d1"], CH1, 2 * m, FT0)
            down_halves(KD - 1, Q["d1"], CH1, 2 * (KD - 1))


def kernel(**inputs):
    import concourse.bacc as bacc
    from concourse.bass_utils import run_bass_kernel_spmd

    v = {k: np.asarray(x) for k, x in inputs.items()}
    p = np.arange(P)
    k_of = 8 * (p[:, None] % 64) + 2 * np.arange(KD)[None, :] + p[:, None] // 64

    def rows(w):
        return np.ascontiguousarray(w.reshape(-1, P, w.shape[1]).transpose(1, 0, 2).reshape(P, -1))

    def pad_f(w):
        w = w.reshape(*w.shape[:-1], 2, -1)
        width = FT0 * P * w.shape[-1] // F0 if w.shape[-1] == F0 else FT0 * 16
        return np.concatenate([w, np.zeros((*w.shape[:-1], width - w.shape[-1]), w.dtype)], axis=-1)

    order = k_of.T.reshape(-1)
    qg = pad_f(v["L0_ffn_qweight_gu"]).reshape(64, 2, FT0, P)
    sg = pad_f(v["L0_ffn_scales_gu"]).reshape(G_GU, 2, FT0, P)
    qd = np.repeat(v["L0_ffn_qweight_down"], 8, axis=0)
    qd = np.concatenate([qd, np.zeros((FT0 * P - F0, D), qd.dtype)]).reshape(FT0, P, KD, P)
    gd = np.concatenate([v["L0_ffn_g_idx_down"], np.zeros(FT0 * P - F0, v["L0_ffn_g_idx_down"].dtype)])
    gu1 = np.stack([v["L1_ffn_gate_w"].reshape(FT1, P, KD, P), v["L1_ffn_up_w"].reshape(FT1, P, KD, P)])
    cst = np.zeros((P, C_END), np.float32)
    cst[:, C_ID:C_ID + P] = np.eye(P)
    cst[:, C_IOTA:C_IOTA + E] = np.arange(E)
    cst[:, C_OGU:C_END] = np.repeat(G_GU * np.arange(FT0), KD)
    arrays = {
        "xT": v["x"].reshape(T, KD, P).transpose(2, 1, 0),
        "wrT": rows(v["L0_cond_Wr"].T).reshape(P, KD, E),
        "aT": rows(v["L0_cond_A"].reshape(E * R, D).T),
        "w0T": rows(v["L0_cond_W"].T[:, order]),
        "bT": v["L0_cond_B"].transpose(0, 2, 1).reshape(E * R, D)[:, order],
        "qw_gu": qg.transpose(2, 0, 1, 3).reshape(FT0, 64, 256),
        "sc_gu": sg.transpose(2, 0, 1, 3).reshape(FT0 * G_GU, 256),
        "qz_gu": pad_f(v["L0_ffn_qzeros_gu"]).reshape(G_GU, -1),
        "qw_dn": qd.transpose(1, 2, 0, 3),
        "sc_dn": v["L0_ffn_scales_down"],
        "qz_dn": v["L0_ffn_qzeros_down"],
        "gidx": np.concatenate([v["L0_ffn_g_idx_gu"][k_of], gd.reshape(FT0, P).T], axis=1),
        "ids": v["itok_B_0_7"],
        "aids": v["itok_B_3_7"],
        "w1T": v["L1_cond_weight"].transpose(0, 2, 1).reshape(NBATCH, KD, P, D).transpose(0, 2, 1, 3).reshape(NBATCH, P, KD * D),
        "lnw": v["L1_ffn_ln_w"].reshape(KD, P).T,
        "gu1": gu1.transpose(1, 4, 3, 0, 2).reshape(FT1, P, KD * 2 * P),
        "d1": v["L1_ffn_down_w"].reshape(KD, P, FT1, P).transpose(0, 3, 2, 1).reshape(KD, P, FT1 * P),
        "cst": cst,
        "shifts": np.stack([4 * (p // 64), 4 * (p % 8)], axis=1).astype(np.uint32),
    }
    nc = bacc.Bacc("TRN2", target_bir_lowering=False, num_devices=1)
    feed, aps = {}, {}
    for name, arr in arrays.items():
        arr = np.ascontiguousarray(arr)
        feed[f"in_{name}"] = arr
        aps[name] = nc.dram_tensor(f"in_{name}", arr.shape, mybir.dt.from_np(arr.dtype), kind="ExternalInput").ap()
    out = nc.dram_tensor("out_T", (KD, P, T), F32, kind="ExternalOutput").ap()
    build(nc, aps, out)
    r = run_bass_kernel_spmd(nc, [feed], core_ids=[0])
    got = r.results[0]["out_T"]
    return got.reshape(D, T).T.reshape(NBATCH, SEQ, D)
```
